# Optimizing a Trainium2 kernel written in Bass

```python
import numpy as np
import jax
import jax.numpy as jnp

def _softmax(x, axis=-1):
    return jax.nn.softmax(x, axis=axis)

def _gelu(x):
    return jax.nn.gelu(x, approximate=True)

def _silu(x):
    return jax.nn.silu(x)

def _sigmoid(x):
    return jax.nn.sigmoid(x)

def _layernorm(x, axis=-1, eps=1e-05):
    m = jnp.mean(x, axis=axis, keepdims=True)
    v = jnp.var(x, axis=axis, keepdims=True)
    return (x - m) / jnp.sqrt(v + eps)

def _scatter_add(tgt, idx, src, axis=0):
    return tgt.at[idx].add(src)

def _segment_sum(src, seg, n):
    return jax.ops.segment_sum(src, seg, n)
kernel_name = 'mk_adj_preln_d2_adj_r2_491a50'

def setup_inputs(seed: int=0):
    np.random.seed(seed)
    _w = jnp.asarray

    def _rec_inputs():
        import jax
        import jax.numpy as jnp
        _gk = jax.random.key(seed)
        x = -0.0002928 + 1 * jax.random.normal(jax.random.fold_in(_gk, 1), (64, 128, 128), jnp.float32)
        _a = jax.random.bernoulli(jax.random.fold_in(_gk, 2), 0.125, (64, 128, 128))
        _a = jnp.logical_or(_a, jnp.swapaxes(_a, -1, -2))
        _a = jnp.logical_or(_a, jnp.eye(128, dtype=bool))
        _af = _a.astype(jnp.float32)
        _af = _af * jax.random.uniform(jax.random.fold_in(_gk, 3), (64, 128, 128), jnp.float32, 0.05, 4.42607)
        adj = _af
        return (x, adj)
    x, adj = _rec_inputs()

    def _L0_gnn_setup():
        import math
        import jax, jax.numpy as jnp
        import numpy as np
        B, N, D, H = (32, 256, 128, 8)
        HD = D // H
        key = jax.random.key(seed)
        ks = jax.random.split(key, 9)
        h = jax.random.normal(ks[0], (B, N, D), dtype=jnp.float32)
        edge = jax.random.normal(ks[1], (B, N, N), dtype=jnp.float32)
        adj = jax.random.uniform(ks[2], (B, N, N)) < 0.5
        adj_mask = adj | jnp.eye(N, dtype=bool)[None]
        s = 1.0 / math.sqrt(D)
        W_q = jax.random.normal(ks[3], (D, D), dtype=jnp.float32) * s
        W_k = jax.random.normal(ks[4], (D, D), dtype=jnp.float32) * s
        W_v = jax.random.normal(ks[5], (D, D), dtype=jnp.float32) * s
        W_e = jax.random.normal(ks[6], (H, 1), dtype=jnp.float32)
        W_o = jax.random.normal(ks[7], (D, D), dtype=jnp.float32) * s
        return {'h': h, 'edge': edge, 'adj_mask': adj_mask, 'W_q': W_q, 'W_k': W_k, 'W_v': W_v, 'W_e': W_e, 'W_o': W_o}
    _L0_gnn_all = _L0_gnn_setup()
    _L0_gnn_in = {k: v for k, v in _L0_gnn_all.items() if k in ('W_q', 'W_k', 'W_v', 'W_e', 'W_o')}
    del _L0_gnn_all

    def _L1_gnn_setup():
        import jax, jax.numpy as jnp
        import numpy as np
        from jax import lax
        DIM = 128
        EPS = 1e-05

        def _bn(h, g, b, m, v):
            scale = g / jnp.sqrt(v + EPS)
            return h * scale[None, :, None] + (b - m * scale)[None, :, None]

        def _conv1d(h, w, pad):
            return lax.conv_general_dilated(h, w, window_strides=(1,), padding=[(pad, pad)], dimension_numbers=('NCH', 'OIH', 'NCH'))
        key = jax.random.key(seed)
        ks = jax.random.split(key, 16)
        bs, n, d = (16, 1024, DIM)
        s = 0.05
        return {'x': jax.random.normal(ks[0], (bs, n, d), jnp.float32), 'mask': jnp.ones((bs, n, n), jnp.float32), 'w_se': jax.random.normal(ks[1], (3, d), jnp.float32) * s, 'b_se': jnp.zeros((3,), jnp.float32), 'conv1_w': jax.random.normal(ks[2], (d, d, 1), jnp.float32) * s, 'bn1_g': jnp.ones((d,), jnp.float32), 'bn1_b': jnp.zeros((d,), jnp.float32), 'bn1_m': jnp.zeros((d,), jnp.float32), 'bn1_v': jnp.ones((d,), jnp.float32), 'conv2_w': jax.random.normal(ks[3], (d, d, 17), jnp.float32) * s, 'bn2_g': jnp.ones((d,), jnp.float32), 'bn2_b': jnp.zeros((d,), jnp.float32), 'bn2_m': jnp.zeros((d,), jnp.float32), 'bn2_v': jnp.ones((d,), jnp.float32), 'w_msg': jax.random.normal(ks[4], (d, d), jnp.float32) * s, 'b_msg': jnp.zeros((d,), jnp.float32), 'w_ih': jax.random.normal(ks[5], (3 * d, 2 * d), jnp.float32) * s, 'b_ih': jnp.zeros((3 * d,), jnp.float32), 'w_hh': jax.random.normal(ks[6], (3 * d, d), jnp.float32) * s, 'b_hh': jnp.zeros((3 * d,), jnp.float32)}
    _L1_gnn_all = _L1_gnn_setup()
    _L1_gnn_in = {k: v for k, v in _L1_gnn_all.items() if k in ('w_se', 'b_se', 'conv1_w', 'bn1_g', 'bn1_b', 'bn1_m', 'bn1_v', 'conv2_w', 'bn2_g', 'bn2_b', 'bn2_m', 'bn2_v', 'w_msg', 'b_msg', 'w_ih', 'b_ih', 'w_hh', 'b_hh')}
    del _L1_gnn_all
    return {'x': x, 'adj': adj, 'L0_gnn_W_q': _L0_gnn_in['W_q'], 'L0_gnn_W_k': _L0_gnn_in['W_k'], 'L0_gnn_W_v': _L0_gnn_in['W_v'], 'L0_gnn_W_e': _L0_gnn_in['W_e'], 'L0_gnn_W_o': _L0_gnn_in['W_o'], 'L1_gnn_w_se': _L1_gnn_in['w_se'], 'L1_gnn_b_se': _L1_gnn_in['b_se'], 'L1_gnn_conv1_w': _L1_gnn_in['conv1_w'], 'L1_gnn_bn1_g': _L1_gnn_in['bn1_g'], 'L1_gnn_bn1_b': _L1_gnn_in['bn1_b'], 'L1_gnn_bn1_m': _L1_gnn_in['bn1_m'], 'L1_gnn_bn1_v': _L1_gnn_in['bn1_v'], 'L1_gnn_conv2_w': _L1_gnn_in['conv2_w'], 'L1_gnn_bn2_g': _L1_gnn_in['bn2_g'], 'L1_gnn_bn2_b': _L1_gnn_in['bn2_b'], 'L1_gnn_bn2_m': _L1_gnn_in['bn2_m'], 'L1_gnn_bn2_v': _L1_gnn_in['bn2_v'], 'L1_gnn_w_msg': _L1_gnn_in['w_msg'], 'L1_gnn_b_msg': _L1_gnn_in['b_msg'], 'L1_gnn_w_ih': _L1_gnn_in['w_ih'], 'L1_gnn_b_ih': _L1_gnn_in['b_ih'], 'L1_gnn_w_hh': _L1_gnn_in['w_hh'], 'L1_gnn_b_hh': _L1_gnn_in['b_hh']}

def reference(x, adj, L0_gnn_W_q, L0_gnn_W_k, L0_gnn_W_v, L0_gnn_W_e, L0_gnn_W_o, L1_gnn_w_se, L1_gnn_b_se, L1_gnn_conv1_w, L1_gnn_bn1_g, L1_gnn_bn1_b, L1_gnn_bn1_m, L1_gnn_bn1_v, L1_gnn_conv2_w, L1_gnn_bn2_g, L1_gnn_bn2_b, L1_gnn_bn2_m, L1_gnn_bn2_v, L1_gnn_w_msg, L1_gnn_b_msg, L1_gnn_w_ih, L1_gnn_b_ih, L1_gnn_w_hh, L1_gnn_b_hh):
    import jax
    import jax.numpy as jnp

    def _L0_gnn_ref(h, edge, adj_mask, W_q, W_k, W_v, W_e, W_o):
        import math
        import jax, jax.numpy as jnp
        import numpy as np
        B, N, D, H = (32, 256, 128, 8)
        HD = D // H
        b, n, _ = h.shape
        q = (h @ W_q.T).reshape(b, n, H, HD).transpose(0, 2, 1, 3)
        k = (h @ W_k.T).reshape(b, n, H, HD).transpose(0, 2, 1, 3)
        v = (h @ W_v.T).reshape(b, n, H, HD).transpose(0, 2, 1, 3)
        edge_bias = jnp.einsum('bij,h->bhij', edge, W_e[:, 0])
        scores = jnp.einsum('bhid,bhjd->bhij', q, k) / math.sqrt(HD) + edge_bias
        scores = jnp.where(adj_mask[:, None], scores, -jnp.inf)
        attn = jax.nn.softmax(scores, axis=-1)
        out = jnp.einsum('bhij,bhjd->bhid', attn, v)
        out = out.transpose(0, 2, 1, 3).reshape(b, n, D)
        return out @ W_o.T

    def _L1_gnn_ref(x, mask, w_se, b_se, conv1_w, bn1_g, bn1_b, bn1_m, bn1_v, conv2_w, bn2_g, bn2_b, bn2_m, bn2_v, w_msg, b_msg, w_ih, b_ih, w_hh, b_hh):
        import jax, jax.numpy as jnp
        import numpy as np
        from jax import lax
        DIM = 128
        EPS = 1e-05

        def _bn(h, g, b, m, v):
            scale = g / jnp.sqrt(v + EPS)
            return h * scale[None, :, None] + (b - m * scale)[None, :, None]

        def _conv1d(h, w, pad):
            return lax.conv_general_dilated(h, w, window_strides=(1,), padding=[(pad, pad)], dimension_numbers=('NCH', 'OIH', 'NCH'))
        d = x.shape[-1]
        xc = jnp.transpose(x, (0, 2, 1))
        h = _bn(_conv1d(xc, conv1_w, 0), bn1_g, bn1_b, bn1_m, bn1_v)
        h = jax.nn.relu(h)
        h = _bn(_conv1d(h, conv2_w, 8), bn2_g, bn2_b, bn2_m, bn2_v)
        x_conv = jnp.transpose(jax.nn.relu(h + xc), (0, 2, 1))
        s = x @ w_se.T + b_se
        sq = jnp.sum(s * s, axis=-1)
        dist = sq[:, :, None] + sq[:, None, :] - 2.0 * jnp.einsum('bnd,bmd->bnm', s, s)
        A = jnp.exp(-dist) * mask
        msg = jax.nn.relu(x @ w_msg.T + b_msg)
        x_nmp = jnp.einsum('bnm,bmd->bnd', A, msg)
        x_in = jnp.concatenate([x_conv, x_nmp], axis=-1)
        gi = x_in @ w_ih.T + b_ih
        gh = x @ w_hh.T + b_hh
        gi_r, gi_z, gi_n = (gi[..., :d], gi[..., d:2 * d], gi[..., 2 * d:])
        gh_r, gh_z, gh_n = (gh[..., :d], gh[..., d:2 * d], gh[..., 2 * d:])
        r = jax.nn.sigmoid(gi_r + gh_r)
        z = jax.nn.sigmoid(gi_z + gh_z)
        nn_ = jnp.tanh(gi_n + r * gh_n)
        return (1.0 - z) * nn_ + z * x
    h = jnp.maximum(_layernorm(x, axis=-1), 0.0)
    x = x + _L0_gnn_ref(h, adj, adj, L0_gnn_W_q, L0_gnn_W_k, L0_gnn_W_v, L0_gnn_W_e, L0_gnn_W_o)
    h = jnp.maximum(_layernorm(x, axis=-1), 0.0)
    x = x + _L1_gnn_ref(h, adj, L1_gnn_w_se, L1_gnn_b_se, L1_gnn_conv1_w, L1_gnn_bn1_g, L1_gnn_bn1_b, L1_gnn_bn1_m, L1_gnn_bn1_v, L1_gnn_conv2_w, L1_gnn_bn2_g, L1_gnn_bn2_b, L1_gnn_bn2_m, L1_gnn_bn2_v, L1_gnn_w_msg, L1_gnn_b_msg, L1_gnn_w_ih, L1_gnn_b_ih, L1_gnn_w_hh, L1_gnn_b_hh)
    return x

_drawn_inputs = setup_inputs


def setup_inputs(seed=0):
    import zlib

    import numpy as np

    out = dict(_drawn_inputs(seed))
    spreads = {'L1_gnn_b_se': (0.0, 0.8),
     'L1_gnn_bn1_g': (1.0, 0.6),
     'L1_gnn_bn1_b': (0.0, 0.755),
     'L1_gnn_bn1_m': (0.0, 0.746),
     'L1_gnn_bn1_v': (1.0, 0.6),
     'L1_gnn_bn2_g': (1.0, 0.6),
     'L1_gnn_bn2_b': (0.0, 0.8),
     'L1_gnn_bn2_m': (0.0, 0.8),
     'L1_gnn_bn2_v': (1.0, 0.6),
     'L1_gnn_b_msg': (0.0, 0.1),
     'L1_gnn_b_ih': (0.0, 0.608),
     'L1_gnn_b_hh': (0.0, 0.76)}
    factors = {}
    for name, (base, spread) in spreads.items():
        noise = np.random.default_rng([zlib.crc32(name.encode()), seed]).standard_normal(out[name].shape)
        drawn = base * np.exp(spread * noise) if base else spread * noise
        out[name] = jnp.asarray(drawn.astype(out[name].dtype))
    for name, factor in factors.items():
        out[name] = (out[name] * factor).astype(out[name].dtype)
    return out
```

```python
from contextlib import ExitStack

import concourse.bass as bass
from concourse import mybir

F32 = mybir.dt.float32
F32R = mybir.dt.float32r
BF16 = mybir.dt.bfloat16
ALU = mybir.AluOpType
ACT = mybir.ActivationFunctionType
AX_X = mybir.AxisListType.X

P = 128
H = 8
HD = P // H
RT = 4
G = 4
TAPS = 17
HALO = TAPS // 2
PADDED = P + 2 * HALO
EPS = 1e-5
MASKED = -(2.0 ** 100)

(W_V, W_O, W_C1, W_MSG, W_IR0, W_IR1, W_IZ0, W_IZ1, W_IN0, W_IN1, W_S, W_HR, W_HZ, W_HN,
 W_TAP) = range(15)
BLOCKS = W_TAP + TAPS
(V_G1, V_B1, V_M1, V_V1, V_G2, V_B2, V_M2, V_V2, V_IH, V_HH) = (0, 1, 2, 3, 4, 5, 6, 7, 8, 11)


def build(nc, x, adj, W_q, W_k, W_v, W_e, W_o, w_se, b_se, conv1_w, bn1_g, bn1_b, bn1_m, bn1_v,
          conv2_w, bn2_g, bn2_b, bn2_m, bn2_v, w_msg, b_msg, w_ih, b_ih, w_hh, b_hh, out):
    NG = x.shape[0] // G
    x_g = x.rearrange("(t b) n d -> t n b d", b=G)
    adj_g = adj.rearrange("(t b) n m -> t n b m", b=G)
    out_g = out.rearrange("(t b) n d -> t n b d", b=G)

    ctx = ExitStack()
    with ctx:
        def sb(name, shape, dt=F32):
            return ctx.enter_context(nc.sbuf_tensor(name, shape, dt))

        def sem(name):
            return ctx.enter_context(nc.semaphore(name))

        ident = sb("ident", [P, P])
        ident_bf = sb("ident_bf", [P, P], BF16)
        low_rows = sb("low_rows", [P, 1])
        eps_t = sb("eps_t", [P, G])
        minus_half = sb("minus_half", [P, G])
        ones2 = sb("ones2", [P, P], F32R)
        wq_n, wk_n, wv_n, wo_n = (sb(f"w{c}_n", [P, P]) for c in "qkvo")
        c1_n = sb("c1_n", [P, P])
        msg_n = sb("msg_n", [P, P])
        ih_n = sb("ih_n", [P, 3, 2 * P])
        hh_n = sb("hh_n", [P, 3, P])
        se_n = sb("se_n", [P, P])
        c2_n = sb("c2_n", [P, P, TAPS])
        vec_n = sb("vec_n", [P, P])
        w_hi = sb("w_hi", [P, BLOCKS, P], F32R)
        w_lo = sb("w_lo", [P, BLOCKS, P], F32R)
        qk_hi = sb("qk_hi", [P, 2, 2, P], F32R)
        qk_lo = sb("qk_lo", [P, 2, 2, P], F32R)
        msg_bias = sb("msg_bias", [P, P], F32R)
        bias_n = sb("bias_n", [P, P])
        bias_r = sb("bias_r", [P, P], F32R)
        vec = sb("vec", [P, 16])
        iv = sb("iv", [P, 2])
        scale12 = sb("scale12", [P, 2])
        ms = sb("ms", [P, 2])
        shift12 = sb("shift12", [P, 2])
        rz_sum = sb("rz_sum", [P, 2])
        rz_bias = sb("rz_bias", [P, 2])
        we = sb("we", [P, H])
        we_n = sb("we_n", [P, H])
        se_bias = sb("se_bias", [P, 1])
        fence = sb("fence", [P, 1])
        xt = sb("xt", [P, 2, G, P])
        xn1 = sb("xn1", [P, G, P])
        st1 = sb("st1", [P, G, 6])
        mv1 = sb("mv1", [P, G, 2])
        ve1 = sb("ve1", [P, G])
        rstd1 = sb("rstd1", [P, G])
        hT_hi = sb("hT_hi", [P, G * P], F32R)
        hT_lo = sb("hT_lo", [P, G * P], F32R)
        q_round = sb("q_round", [P, 2, G * P], F32R)
        Q = sb("Q", [P, 2, 2, G, P], F32R)
        K_hi = sb("K_hi", [P, 2, 2, G, P], F32R)
        K_lo = sb("K_lo", [P, 2, 2, G, P], F32R)
        v_aug = sb("v_aug", [P, 2, G, H, HD + 1])
        adj_t = sb("adj_t", [P, 2, G, P])
        neg = sb("neg", [P, G, P], BF16)
        prob = sb("prob", [P, G, H, P])
        smax = sb("smax", [P, G, H])
        probT = sb("probT", [P, 2, H, P])
        rden = sb("rden", [P, 2 * H])
        attn = sb("attn", [P, G, P])
        aT_hi = sb("aT_hi", [P, G * P], F32R)
        aT_lo = sb("aT_lo", [P, G * P], F32R)
        xr = sb("xr", [P, G, P])
        x2 = sb("x2", [P, 2, G, P])
        xn2 = sb("xn2", [P, G, P])
        st2 = sb("st2", [P, G, 6])
        mv2 = sb("mv2", [P, G, 2])
        ve2 = sb("ve2", [P, G])
        rstd2 = sb("rstd2", [P, G])
        h2_hi = sb("h2_hi", [P, G * P], F32R)
        h2_lo = sb("h2_lo", [P, G * P], F32R)
        h2 = sb("h2", [P, G * P])
        res = sb("res", [P, G * P])
        h1 = sb("h1", [P, G, P])
        h1_hi = sb("h1_hi", [P, G, PADDED], F32R)
        h1_lo = sb("h1_lo", [P, G, PADDED], F32R)
        U = sb("U", [P, G, P])
        V = sb("V", [P, G, P])
        msg = sb("msg", [P, G, P])
        near = sb("near", [P, G * P])
        AT = sb("AT", [P, G, P])
        y = sb("y", [P, G * P])
        c_hi = sb("c_hi", [P, G * P], F32R)
        c_lo = sb("c_lo", [P, G * P], F32R)
        n_hi = sb("n_hi", [P, G * P], F32R)
        n_lo = sb("n_lo", [P, G * P], F32R)
        rz = sb("rz", [P, 2, G * P])
        ghn = sb("ghn", [P, G * P])
        rg = sb("rg", [P, G * P])
        cand = sb("cand", [P, G * P])
        nn = sb("nn", [P, G * P])
        hn = sb("hn", [P, G * P])
        oT = sb("oT", [P, G, P])
        out_t = sb("out_t", [P, 2, G, P])

        ps_s = ctx.enter_context(nc.psum_tensor("ps_s", [P, RT, 512], F32))
        ps_t = ctx.enter_context(nc.psum_tensor("ps_t", [P, 2, 512], F32))
        ps6 = ctx.enter_context(nc.psum_tensor("ps6", [P, 512], F32))
        ps7 = ctx.enter_context(nc.psum_tensor("ps7", [P, 512], F32))

        ld_vec, ld_qk, ld_w1, ld_w2, ld_c2 = (sem(f"ld_{n}") for n in ("vec", "qk", "w1", "w2", "c2"))
        x_in = [sem("x_in0"), sem("x_in1")]
        adj_in = [sem("adj_in0"), sem("adj_in1")]
        xr_in, out_st = sem("xr_in"), [sem("out_st0"), sem("out_st1")]
        const_made, ident_made, zeros_made = sem("const_made"), sem("ident_made"), sem("zeros_made")
        dve_setup, su_full, su_hi, su_done = sem("dve_setup"), sem("su_full"), sem("su_hi"), sem("su_done")
        iv_ready, params_ready = sem("iv_ready"), sem("params_ready")
        iv_sum = sem("iv_sum")
        (h2T_full, hT_full, conv1_full, s_full, msg_full, dist_full, adjT_full, v_full, conv2_full,
         outT_full, nmp_full, av_full, ghn_full, attnT_full, r_full, wo_full, z_full, gin_full,
         scores_full, probT_full) = (sem(n + "_full") for n in (
             "h2T", "hT", "conv1", "s", "msg", "dist", "adjT", "v", "conv2", "outT", "nmp", "av",
             "ghn", "attnT", "r", "wo", "z", "gin", "scores", "probT"))
        qk_full = [sem(f"{n}_full") for n in ("q0", "q1", "k0", "k1")]
        (h2_hi_made, hT_hi_made, h1_made, uv_made, msg_made, near_made, v_made, exp_made,
         probT_made, n_hi_made, c_hi_made, ghn_made, aT_hi_made, r_tanh_made, z_tanh_made,
         nn_made) = (sem(n + "_made") for n in (
             "h2_hi", "hT_hi", "h1", "uv", "msg", "near", "v", "exp", "probT", "n_hi", "c_hi",
             "ghn", "aT_hi", "r_tanh", "z_tanh", "nn"))
        qk_round = [sem(f"{n}_round") for n in ("q0", "q1", "k0", "k1")]
        (out_made, h2_lo_made, hT_lo_made, edge_added, max_made, shifted, mask_made, AT_made,
         rden_made, attn_made, n_lo_made, y_made, c_lo_made, aT_lo_made, x2_made, r_made, z_made,
         cand_made, xn1_made, xn2_made, stats1, moments1, stats2, moments2) = (
             sem(n) for n in (
                 "out_made", "h2_lo_made", "hT_lo_made", "edge_added", "max_made", "shifted",
                 "mask_made", "AT_made", "rden_made", "attn_made", "n_lo_made", "y_made",
                 "c_lo_made", "aT_lo_made", "x2_made", "r_made", "z_made", "cand_made",
                 "xn1_made", "xn2_made", "stats1", "moments1", "stats2", "moments2"))
        qk_split = [sem(f"{n}_split") for n in ("q0", "q1", "k0", "k1")]
        (edge_made, h2_made, res_made, h1_lo_made, var1_made, rstd1_made, var2_made, rstd2_made,
         rg_made, hn_made, zhn_made, oT_made) = (sem(n) for n in (
             "edge_made", "h2_made", "res_made", "h1_lo_made", "var1_made", "rstd1_made",
             "var2_made", "rstd2_made", "rg_made", "hn_made", "zhn_made", "oT_made"))

        def groups(eng, s, g, each=1):
            if isinstance(g, int):
                g = min(g, NG - 1)
                if g < 0:
                    return
            eng.wait_ge(s, g * each + each)

        def count(eng, s, n):
            if not isinstance(n, int) or n > 0:
                eng.wait_ge(s, n)

        def landed(eng, pair, g, parity):
            eng.wait_ge(pair[parity], (g - parity) * 8 + 16)

        def has(g):
            return not isinstance(g, int) or 0 <= g < NG

        def run(eng, step):
            for t in range(-2, 2):
                step(t, t % 2)
            with eng.Fori(0, (NG - 4) // 2) as i:
                step(2 * i + 2, 0)
                step(2 * i + 3, 1)
            for t in range(NG - 2, NG + 2):
                step(t, t % 2)

        block_src = {W_V: wv_n[:, :], W_O: wo_n[:, :], W_C1: c1_n[:, :], W_MSG: msg_n[:, :],
                     W_S: se_n[:, :], W_HR: hh_n[:, 0, :], W_HZ: hh_n[:, 1, :], W_HN: hh_n[:, 2, :]}
        for gate, first in enumerate((W_IR0, W_IZ0, W_IN0)):
            for part in range(2):
                block_src[first + part] = ih_n[:, gate, part * P:(part + 1) * P]
        for tap in range(TAPS):
            block_src[W_TAP + tap] = c2_n[:, :, tap]
        batches = [range(b, min(b + 4, BLOCKS)) for b in range(0, BLOCKS, 4)]
        LD_VEC = 19
        SU = 3 + len(batches)

        block = ctx.enter_context(nc.Block())

        @block.sync
        def _(sp):
            sp.dma_start(xt[:, 0], x_g[0]).then_inc(x_in[0], 16)
            sp.dma_start(wq_n[:, :], W_q).then_inc(ld_qk, 16)
            sp.dma_start(wk_n[:, :], W_k).then_inc(ld_qk, 16)
            sp.wait_ge(zeros_made, 1)
            for row, v in ((V_G1, bn1_g), (V_B1, bn1_b), (V_M1, bn1_m), (V_V1, bn1_v),
                           (V_G2, bn2_g), (V_B2, bn2_b), (V_M2, bn2_m), (V_V2, bn2_v)):
                sp.dma_start(vec_n[row:row + 1, :], v.unsqueeze(0)).then_inc(ld_vec, 16)
            for row, v in ((V_IH, b_ih), (V_HH, b_hh)):
                sp.dma_start(vec_n[row:row + 3, :], v.rearrange("(g o) -> g o", o=P)).then_inc(ld_vec, 16)
            for row in (0, 32, 64):
                sp.dma_start(se_n[row:row + 3, :], w_se).then_inc(ld_vec, 16)
                sp.dma_start(se_bias[row:row + 3, :], b_se.unsqueeze(1)).then_inc(ld_vec, 16)
            for row in (0, 32):
                sp.dma_start(bias_n[row:row + 1, :], b_msg.unsqueeze(0)).then_inc(ld_vec, 16)
            sp.dma_start(we_n[:, :], W_e.rearrange("h o -> o h").to_broadcast([P, H])).then_inc(ld_vec, 16)
            sp.dma_start(adj_t[:, 0], adj_g[0]).then_inc(adj_in[0], 16)
            for n, w in ((wv_n[:, :], W_v), (wo_n[:, :], W_o),
                         (c1_n[:, :], conv1_w.rearrange("o i k -> o (i k)")), (msg_n[:, :], w_msg)):
                sp.dma_start(n, w).then_inc(ld_w1, 16)
            sp.dma_start(xt[:, 1], x_g[1]).then_inc(x_in[1], 16)
            sp.dma_start(ih_n[:, :, :], w_ih.rearrange("(g o) c -> o g c", o=P)).then_inc(ld_w2, 16)
            sp.dma_start(hh_n[:, :, :], w_hh.rearrange("(g o) c -> o g c", o=P)).then_inc(ld_w2, 16)
            sp.dma_start(c2_n[:, :, :], conv2_w).then_inc(ld_c2, 16)

            def step(t, q):
                if has(t + 1) and not (isinstance(t, int) and t == -1):
                    groups(sp, adjT_full, t - 1)
                    groups(sp, mask_made, t - 1)
                    groups(sp, edge_made, t - 1, G)
                    sp.dma_start(adj_t[:, 1 - q], adj_g[t + 1]).then_inc(adj_in[1 - q], 16)
                if has(t) and has(t + 2):
                    groups(sp, xn1_made, t)
                    sp.dma_start(xt[:, q], x_g[t + 2]).then_inc(x_in[q], 16)
                if has(t):
                    groups(sp, x2_made, t - 1)
                    sp.dma_start(xr[:, :, :], x_g[t]).then_inc(xr_in, 16)
                if has(t - 2):
                    groups(sp, out_made, t - 2)
                    sp.dma_start(out_g[t - 2], out_t[:, q]).then_inc(out_st[q], 16)

            run(sp, step)
            for q in range(2):
                sp.wait_ge(out_st[q], 16 * (NG // 2))

        @block.gpsimd
        def _(gp):
            gp.memset(ident[:, :], 0.0).then_inc(ident_made, 1)
            gp.memset(vec_n[:, :], 0.0)
            gp.memset(se_n[:, :], 0.0)
            gp.memset(se_bias[:, :], 0.0)
            gp.memset(bias_n[:, :], 0.0).then_inc(zeros_made, 1)
            gp.wait_ge(ident_made, 1)
            gp.affine_select(out=ident[:, :], in_=ident[:, :], compare_op=ALU.not_equal, fill=1.0,
                             base=0, pattern=[[-1, P]], channel_multiplier=1).then_inc(ident_made, 1)
            gp.memset(eps_t[:, :], EPS)
            gp.memset(minus_half[:, :], -0.5)
            gp.memset(v_aug[:, :, :, :, :].rearrange("p a b c d -> p (a b c d)"), 1.0)
            gp.memset(U[:, :, :], 0.0)
            gp.memset(V[:, :, :], 0.0)
            gp.memset(h1_hi[:, :, :].bitcast(F32), 0.0)
            gp.memset(h1_lo[:, :, :].bitcast(F32), 0.0)
            gp.memset(msg_bias[:, :].bitcast(F32), 0.0)
            gp.memset(ones2[:, :].bitcast(F32), 0.0).then_inc(ident_made, 1)
            gp.wait_ge(ident_made, 3)
            gp.memset(U[64:67, :, :], -0.5)
            gp.memset(V[32:35, :, :], -0.5)
            gp.memset(ones2[0:1, :].bitcast(F32), 1.0)
            gp.memset(ones2[32:33, :].bitcast(F32), 1.0).then_inc(const_made, 1)
            gp.wait_ge(const_made, 1)

            def rstd(mv, ve, out_, moments, var_made, made, g):
                groups(gp, moments, g)
                gp.tensor_tensor(ve[:, :], mv[:, :, 1], eps_t[:, :], ALU.add).then_inc(var_made, 1)
                groups(gp, var_made, g)
                gp.tensor_tensor(out_[:, :], ve[:, :], minus_half[:, :], ALU.pow).then_inc(made, 1)

            def edge(g, b, parity):
                gp.tensor_tensor(prob[:, b], adj_t[:, parity, b].unsqueeze(1).broadcast_to([P, H, P]),
                                 we[:, :].unsqueeze(2).broadcast_to([P, H, P]), ALU.mult
                                 ).then_inc(edge_made, 1)

            def step(t, q):
                l = t - 1
                if has(l):
                    groups(gp, h2_lo_made, l)
                    gp.tensor_tensor(h2[:, :], h2_hi[:, :].bitcast(F32), h2_lo[:, :].bitcast(F32),
                                     ALU.add).then_inc(h2_made, 1)
                    groups(gp, h2_made, l)
                    groups(gp, y_made, l - 1)
                    gp.tensor_tensor(res[:, :], h2[:, :], shift12[:, 1:2].to_broadcast([P, G * P]),
                                     ALU.add).then_inc(res_made, 1)
                    groups(gp, h1_made, l)
                    groups(gp, conv2_full, l - 1)
                    gp.tensor_tensor(h1_lo[:, :, HALO:HALO + P], h1[:, :, :],
                                     h1_hi[:, :, HALO:HALO + P].bitcast(F32), ALU.subtract
                                     ).then_inc(h1_lo_made, 1)
                if isinstance(t, int) and t == -2:
                    rstd(mv1, ve1, rstd1, moments1, var1_made, rstd1_made, 0)
                    return
                if has(t + 1):
                    landed(gp, adj_in, t + 1, 1 - q)
                    for b in range(G):
                        count(gp, probT_full, t * (2 * G) + (2 * b + 2) if has(t) else 0)
                        edge(t + 1, b, 1 - q)
                if has(t):
                    rstd(mv2, ve2, rstd2, moments2, var2_made, rstd2_made, t)
                if has(t + 2):
                    rstd(mv1, ve1, rstd1, moments1, var1_made, rstd1_made, t + 2)
                if has(l):
                    groups(gp, ghn_made, l)
                    groups(gp, r_made, l)
                    groups(gp, cand_made, l - 1)
                    gp.tensor_tensor(rg[:, :], ghn[:, :], rz[:, 0], ALU.mult).then_inc(rg_made, 1)
                    groups(gp, nn_made, l)
                    gp.tensor_tensor(hn[:, :], h2[:, :], nn[:, :], ALU.subtract).then_inc(hn_made, 1)
                    groups(gp, hn_made, l)
                    groups(gp, z_made, l)
                    gp.tensor_tensor(hn[:, :], hn[:, :], rz[:, 1], ALU.mult).then_inc(zhn_made, 1)
                    groups(gp, zhn_made, l)
                    groups(gp, outT_full, l - 1)
                    gp.tensor_tensor(oT[:, :, :].rearrange("p b n -> p (b n)"), hn[:, :], nn[:, :],
                                     ALU.add).then_inc(oT_made, 1)

            gp.wait_ge(su_hi, 3)
            gp.tensor_tensor(iv[:, :], vec[:, V_V1:V_V2 + 1:4], eps_t[:, 0:2], ALU.add).then_inc(iv_sum, 1)
            gp.wait_ge(iv_sum, 1)
            gp.tensor_tensor(iv[:, :], iv[:, :], minus_half[:, 0:2], ALU.pow).then_inc(iv_ready, 1)
            gp.wait_ge(params_ready, 1)
            run(gp, step)

        @block.scalar
        def _(act):
            for n in range(SU):
                act.wait_ge(su_full, n + 1)
                src = ps_t[:, n % 2, :]
                if n < 2:
                    for rep in range(2):
                        dst = qk_hi[:, n].rearrange("p f (r s d) -> p (f r) s d", s=2, d=HD)[:, :, rep]
                        last = nc.scalar.activation(dst, src[:, 0:P].rearrange("p (a d) -> p a d", d=HD),
                                                    ACT.Copy, scale=0.25 if n == 0 else 1.0)
                    last.then_inc(su_hi, 1)
                elif n == 2:
                    nc.scalar.activation(vec[:, :], src[:, 0:16], ACT.Copy).then_inc(su_hi, 1)
                else:
                    bl = batches[n - 3]
                    nc.scalar.activation(w_hi[:, bl[0]:bl[-1] + 1, :].rearrange("p a b -> p (a b)"),
                                         src[:, 0:len(bl) * P], ACT.Copy).then_inc(su_hi, 1)
            act.wait_ge(params_ready, 1)
            act.wait_ge(const_made, 1)

            def step(t, q):
                l, p = t - 1, t + 1
                if has(l):
                    groups(act, h2T_full, l)
                    groups(act, z_full, l - 1)
                    groups(act, h2_made, l - 1)
                    nc.scalar.activation(h2_hi[:, :], ps6[:, :], ACT.Relu).then_inc(h2_hi_made, 1)
                if has(p):
                    groups(act, hT_full, p)
                    groups(act, v_full, p - 1)
                    nc.scalar.activation(hT_hi[:, :], ps7[:, :], ACT.Relu).then_inc(hT_hi_made, 1)
                if has(l):
                    groups(act, conv1_full, l)
                    groups(act, h1_lo_made, l - 1)
                    groups(act, conv2_full, l - 1)
                    nc.scalar.activation(h1[:, :, :].rearrange("p b n -> p (b n)"), ps6[:, :], ACT.Relu,
                                         bias=shift12[:, 0:1], scale=scale12[:, 0:1])
                    nc.scalar.activation(h1_hi[:, :, HALO:HALO + P], ps6[:, :].rearrange("p (b n) -> p b n", b=G),
                                         ACT.Relu, bias=shift12[:, 0:1], scale=scale12[:, 0:1]
                                         ).then_inc(h1_made, 1)

                def round_qk(n):
                    if not has(p):
                        return
                    groups(act, qk_full[n], p)
                    if n < 2:
                        groups(act, qk_split[n], p - 1)
                        dst = q_round[:, n]
                    else:
                        groups(act, scores_full, p - 2, 2)
                        dst = K_hi[:, 1 - q, n - 2].rearrange("p b n -> p (b n)")
                    nc.scalar.activation(dst, ps7[:, :], ACT.Copy).then_inc(qk_round[n], 1)

                round_qk(0)
                if has(l):
                    groups(act, s_full, l)
                    groups(act, dist_full, l - 1)
                    for dst, row, f in ((U, 0, ACT.Identity), (V, 0, ACT.Identity),
                                        (U, 32, ACT.Square), (V, 64, ACT.Square)):
                        last = nc.scalar.activation(dst[row:row + 3, :, :].rearrange("p b n -> p (b n)"),
                                                    ps6[row:row + 3, :], f, bias=se_bias[row:row + 3, :])
                    last.then_inc(uv_made, 1)
                round_qk(1)
                if has(l):
                    groups(act, msg_full, l)
                    groups(act, nmp_full, l - 1)
                    nc.scalar.activation(msg[:, :, :].rearrange("p b n -> p (b n)"), ps6[:, :], ACT.Relu
                                         ).then_inc(msg_made, 1)
                round_qk(2)
                if has(l):
                    groups(act, dist_full, l)
                    groups(act, AT_made, l - 1)
                    nc.scalar.activation(near[:, :], ps6[:, :], ACT.Exp, scale=2.0).then_inc(near_made, 1)
                round_qk(3)
                if has(p):
                    groups(act, v_full, p)
                    groups(act, av_full, p - 2, G)
                    nc.scalar.activation(v_aug[:, 1 - q, :, :, 0:HD].rearrange("p b h d -> p (b h) d"),
                                         ps7[:, :].rearrange("p (a d) -> p a d", d=HD), ACT.Copy
                                         ).then_inc(v_made, 1)

                def exp(b):
                    if not has(t):
                        return
                    count(act, shifted, t * G + b + 1)
                    e = prob[:, b].rearrange("p h n -> p (h n)")
                    nc.scalar.activation(e, e, ACT.Exp).then_inc(exp_made, 1)

                def copy_probT(b):
                    if not has(t):
                        return
                    count(act, av_full, t * G + (b - 1))
                    for k in range(2):
                        count(act, probT_full, t * (2 * G) + (2 * b + k + 1))
                        nc.scalar.activation(probT[:, b % 2, 4 * k:4 * k + 4].rearrange("p h n -> p (h n)"),
                                             ps_t[:, k, :], ACT.Copy).then_inc(probT_made, 1)

                exp(0)
                if has(l):
                    groups(act, nmp_full, l)
                    groups(act, gin_full, l - 1)
                    nc.scalar.activation(n_hi[:, :], ps7[:, :], ACT.Copy).then_inc(n_hi_made, 1)
                copy_probT(0)
                exp(1)
                copy_probT(1)
                exp(2)
                copy_probT(2)
                exp(3)
                copy_probT(3)
                if has(l):
                    groups(act, y_made, l)
                    groups(act, gin_full, l - 1)
                    nc.scalar.activation(c_hi[:, :], y[:, :], ACT.Relu).then_inc(c_hi_made, 1)
                    groups(act, ghn_full, l)
                    groups(act, rg_made, l - 1)
                    nc.scalar.activation(ghn[:, :], ps7[:, :], ACT.Identity,
                                         bias=vec[:, V_HH + 2:V_HH + 3]).then_inc(ghn_made, 1)
                if has(t):
                    groups(act, attnT_full, t)
                    groups(act, wo_full, t - 1)
                    nc.scalar.activation(aT_hi[:, :], ps6[:, :], ACT.Copy).then_inc(aT_hi_made, 1)
                if has(l):
                    groups(act, oT_made, l - 1)
                    groups(act, r_full, l)
                    nc.scalar.activation(rz[:, 0], ps7[:, :], ACT.Tanh, bias=rz_bias[:, 0:1], scale=0.5
                                         ).then_inc(r_tanh_made, 1)
                    groups(act, z_full, l)
                    nc.scalar.activation(rz[:, 1], ps7[:, :], ACT.Tanh, bias=rz_bias[:, 1:2], scale=0.5
                                         ).then_inc(z_tanh_made, 1)
                    groups(act, cand_made, l)
                    nc.scalar.activation(nn[:, :], cand[:, :], ACT.Tanh, bias=vec[:, V_IH + 2:V_IH + 3]
                                         ).then_inc(nn_made, 1)

            run(act, step)

        @block.vector
        def _(dve):
            V_ = nc.vector
            dve.wait_ge(ident_made, 2)
            V_.tensor_copy(ident_bf[:, :], ident[:, :])
            V_.tensor_reduce(
                low_rows[:, :], ident[:, :].rearrange("p (r s d) -> p r s d", s=2, d=HD)[:, :, 1],
                mybir.AxisListType.XY, ALU.add, negate=True).then_inc(dve_setup, 1)
            for n in range(SU):
                dve.wait_ge(su_hi, n + 1)
                src = ps_t[:, n % 2, :]
                if n < 2:
                    for rep in range(2):
                        hi = qk_hi[:, n].rearrange("p f (r s d) -> p (f r) s d", s=2, d=HD)[:, :, rep]
                        lo = qk_lo[:, n].rearrange("p f (r s d) -> p (f r) s d", s=2, d=HD)[:, :, rep]
                        last = V_.scalar_tensor_tensor(lo, src[:, 0:P].rearrange("p (a d) -> p a d", d=HD),
                                                       0.25 if n == 0 else 1.0, hi.bitcast(F32),
                                                       ALU.mult, ALU.subtract)
                    last.then_inc(su_done, 1)
                elif n == 2:
                    dve.wait_ge(iv_ready, 1)
                    V_.tensor_tensor(rz_sum[:, :], vec[:, V_IH:V_IH + 2], vec[:, V_HH:V_HH + 2], ALU.add)
                    V_.tensor_tensor(scale12[:, :], vec[:, V_G1:V_G2 + 1:4], iv[:, :], ALU.mult).then_inc(dve_setup, 1)
                    dve.wait_ge(dve_setup, 2)
                    V_.tensor_scalar(rz_bias[:, :], rz_sum[:, :], 0.5, None, ALU.mult)
                    V_.tensor_tensor(ms[:, :], vec[:, V_M1:V_M2 + 1:4], scale12[:, :], ALU.mult).then_inc(dve_setup, 1)
                    dve.wait_ge(ld_vec, 16 * LD_VEC)
                    dve.wait_ge(const_made, 1)
                    V_.tensor_copy(we[:, :].rearrange("p (r f) -> p r f", f=2),
                                   we_n[:, :].rearrange("p (f r) -> p r f", f=2))
                    V_.tensor_copy(msg_bias[0:1, :], bias_n[0:1, :])
                    V_.tensor_copy(bias_r[32:33, :], bias_n[32:33, :]).then_inc(dve_setup, 1)
                    dve.wait_ge(dve_setup, 4)
                    V_.tensor_tensor(msg_bias[32:33, :], bias_n[32:33, :], bias_r[32:33, :].bitcast(F32), ALU.subtract)
                    V_.tensor_tensor(shift12[:, :], vec[:, V_B1:V_B2 + 1:4], ms[:, :], ALU.subtract
                                     ).then_inc(params_ready, 1)
                    V_.memset(fence[:, :], 0.0).then_inc(su_done, 1)
                else:
                    bl = batches[n - 3]
                    hi, lo = (w[:, bl[0]:bl[-1] + 1, :].rearrange("p a b -> p (a b)") for w in (w_hi, w_lo))
                    V_.tensor_tensor(lo, src[:, 0:len(bl) * P], hi.bitcast(F32), ALU.subtract).then_inc(su_done, 1)

            def moments(src, st, mv, stats, made, g):
                for b in range(G):
                    V_.bn_stats(st[:, b], src[:, b]).then_inc(stats, 1)
                groups(dve, stats, g, G)
                V_.memset(fence[:, :], 0.0)
                for b in range(G):
                    last = V_.bn_aggr(mv[:, b], st[:, b])
                last.then_inc(made, 1)

            def normalise(dst, src, mv, rs, made):
                for b in range(G):
                    last = V_.tensor_scalar(dst[:, b], src[:, b], mv[:, b, 0:1], rs[:, b:b + 1],
                                            ALU.subtract, ALU.mult)
                last.then_inc(made, 1)

            def layernorm1(g, parity):
                landed(dve, x_in, g, parity)
                groups(dve, rstd1_made, g - 1)
                moments(xt[:, parity], st1, mv1, stats1, moments1, g)
                groups(dve, rstd1_made, g)
                groups(dve, hT_full, g - 1)
                normalise(xn1, xt[:, parity], mv1, rstd1, xn1_made)

            def mask(g, parity):
                landed(dve, adj_in, g, parity)
                V_.tensor_scalar(neg[:, :, :], adj_t[:, parity], 0.0, MASKED, ALU.is_equal, ALU.mult
                                 ).then_inc(mask_made, 1)

            def step(t, q):
                l, p = t - 1, t + 1
                first = isinstance(t, int) and t == -2
                if first:
                    layernorm1(0, 0)
                    return
                if has(l):
                    groups(dve, h2_hi_made, l)
                    groups(dve, z_full, l - 1)
                    groups(dve, h2_made, l - 1)
                    V_.scalar_tensor_tensor(h2_lo[:, :], ps6[:, :], 0.0, h2_hi[:, :].bitcast(F32),
                                            ALU.max, ALU.subtract).then_inc(h2_lo_made, 1)
                if has(p):
                    groups(dve, hT_hi_made, p)
                    groups(dve, v_full, p - 1)
                    V_.scalar_tensor_tensor(hT_lo[:, :], ps7[:, :], 0.0, hT_hi[:, :].bitcast(F32),
                                            ALU.max, ALU.subtract).then_inc(hT_lo_made, 1)

                def add_edges(u):
                    if not has(t):
                        return
                    count(dve, scores_full, t * 2 + (u + 1))
                    for b in (2 * u, 2 * u + 1):
                        count(dve, edge_made, t * G + (b + 1))
                        e = prob[:, b].rearrange("p (r f) n -> p r (f n)", f=2)
                        V_.tensor_tensor(e, ps_s[:, :, 256 * (b % 2):256 * (b % 2) + 256], e, ALU.add
                                         ).then_inc(edge_added, 1)

                def split_qk(n):
                    if not has(p):
                        return
                    groups(dve, qk_round[n], p)
                    groups(dve, scores_full, p - 2, 2)
                    if n < 2:
                        V_.scalar_tensor_tensor(Q[:, 1 - q, n].rearrange("p b n -> p (b n)"),
                                                q_round[:, n].bitcast(F32), low_rows[:, 0:1], ps7[:, :],
                                                ALU.mult, ALU.add).then_inc(qk_split[n], 1)
                    else:
                        hi, lo = (K[:, 1 - q, n - 2].rearrange("p b n -> p (b n)") for K in (K_hi, K_lo))
                        V_.tensor_tensor(lo, ps7[:, :], hi.bitcast(F32), ALU.subtract
                                         ).then_inc(qk_split[n], 1)

                def row_max(b):
                    if has(t):
                        count(dve, edge_added, t * G + (b + 1))
                        V_.reduce_max(smax[:, b], prob[:, b], AX_X).then_inc(max_made, 1)

                def shift(b):
                    if has(t):
                        count(dve, max_made, t * G + (b + 1))
                        V_.tensor_tensor(prob[:, b], prob[:, b], smax[:, b].unsqueeze(2).broadcast_to([P, H, P]),
                                         ALU.subtract).then_inc(shifted, 1)

                def norm_attn(u):
                    if not has(t):
                        return
                    count(dve, av_full, t * G + (2 * u + 2))
                    av = ps7[:, 0:2 * H * (HD + 1)].rearrange("p (a d) -> p a d", d=HD + 1)
                    count(dve, attn_made, t * 2 + u)
                    V_.reciprocal(rden[:, :], av[:, :, HD]).then_inc(rden_made, 1)
                    count(dve, rden_made, t * 2 + (u + 1))
                    groups(dve, attnT_full, t - 1)
                    V_.tensor_tensor(attn[:, 2 * u:2 * u + 2].rearrange("p b (h d) -> p (b h) d", d=HD),
                                     av[:, :, 0:HD], rden[:, :].unsqueeze(2).broadcast_to([P, 2 * H, HD]),
                                     ALU.mult).then_inc(attn_made, 1)

                add_edges(0)
                split_qk(0)
                row_max(0)
                split_qk(1)
                shift(0)
                split_qk(2)
                row_max(1)
                split_qk(3)
                shift(1)
                add_edges(1)
                if has(l):
                    groups(dve, near_made, l)
                    groups(dve, adjT_full, l)
                    groups(dve, nmp_full, l - 1)
                    V_.tensor_tensor(AT[:, :, :].rearrange("p b n -> p (b n)"), ps6[:, :], near[:, :],
                                     ALU.mult).then_inc(AT_made, 1)
                row_max(2)
                if has(t - 2):
                    groups(dve, outT_full, t - 2)
                    count(dve, out_st[q], (t - 2 - q) * 8)
                    V_.tensor_tensor(out_t[:, q].rearrange("p b n -> p (b n)"), ps7[:, :],
                                     x2[:, q].rearrange("p b n -> p (b n)"), ALU.add).then_inc(out_made, 1)
                shift(2)
                if has(l):
                    groups(dve, n_hi_made, l)
                    groups(dve, gin_full, l - 1)
                    V_.tensor_tensor(n_lo[:, :], ps7[:, :], n_hi[:, :].bitcast(F32), ALU.subtract
                                     ).then_inc(n_lo_made, 1)
                row_max(3)
                shift(3)
                norm_attn(0)
                if has(p):
                    groups(dve, scores_full, t, 2)
                    mask(p, 1 - q)
                norm_attn(1)
                if has(l):
                    groups(dve, conv2_full, l)
                    groups(dve, res_made, l)
                    groups(dve, c_hi_made, l - 1)
                    V_.scalar_tensor_tensor(y[:, :], ps6[:, :], scale12[:, 1:2], res[:, :], ALU.mult, ALU.add
                                            ).then_inc(y_made, 1)
                    groups(dve, c_hi_made, l)
                    groups(dve, gin_full, l - 1)
                    V_.scalar_tensor_tensor(c_lo[:, :], y[:, :], 0.0, c_hi[:, :].bitcast(F32),
                                            ALU.max, ALU.subtract).then_inc(c_lo_made, 1)
                if has(t):
                    groups(dve, aT_hi_made, t)
                    groups(dve, wo_full, t - 1)
                    V_.tensor_tensor(aT_lo[:, :], ps6[:, :], aT_hi[:, :].bitcast(F32), ALU.subtract
                                     ).then_inc(aT_lo_made, 1)
                if has(l):
                    groups(dve, r_tanh_made, l)
                    V_.tensor_scalar(rz[:, 0], rz[:, 0], 0.5, 0.5, ALU.mult, ALU.add).then_inc(r_made, 1)
                if has(t):
                    groups(dve, wo_full, t)
                    dve.wait_ge(xr_in, t * 16 + 16)
                    V_.tensor_tensor(x2[:, q].rearrange("p b n -> p (b n)"), ps6[:, :],
                                     xr[:, :, :].rearrange("p b n -> p (b n)"), ALU.add).then_inc(x2_made, 1)
                    groups(dve, x2_made, t)
                    moments(x2[:, q], st2, mv2, stats2, moments2, t)
                if has(l):
                    groups(dve, z_tanh_made, l)
                    V_.tensor_scalar(rz[:, 1], rz[:, 1], 0.5, 0.5, ALU.mult, ALU.add).then_inc(z_made, 1)
                if has(t):
                    groups(dve, rstd2_made, t)
                    groups(dve, h2T_full, t - 1)
                    normalise(xn2, x2[:, q], mv2, rstd2, xn2_made)
                if has(t + 2):
                    layernorm1(t + 2, q)
                if has(l):
                    groups(dve, rg_made, l)
                    groups(dve, gin_full, l)
                    groups(dve, nn_made, l - 1)
                    V_.tensor_tensor(cand[:, :], ps6[:, :], rg[:, :], ALU.add).then_inc(cand_made, 1)

            run(dve, step)

        @block.tensor
        def _(pe):
            mm = nc.tensor.matmul

            pe.wait_ge(ident_made, 2)
            for n in range(SU):
                if n >= 2:
                    pe.wait_ge(su_done, n - 1)
                if n == 0:
                    pe.wait_ge(ld_qk, 32)
                if n == 2:
                    pe.wait_ge(ld_vec, 16 * LD_VEC)
                if n == 3:
                    pe.wait_ge(ld_w1, 64)
                if n == 4:
                    pe.wait_ge(ld_w2, 32)
                if n >= 3 and W_TAP in batches[n - 3]:
                    pe.wait_ge(ld_c2, 16)
                src = {0: [wq_n[:, :]], 1: [wk_n[:, :]], 2: [vec_n[:, :]]}.get(n) or [
                    block_src[i] for i in batches[n - 3]]
                for i, w in enumerate(src):
                    last = nc.tensor.transpose(ps_t[:, n % 2, i * P:(i + 1) * P], w, ident[:, :])
                last.then_inc(su_full, 1)
            pe.wait_ge(su_done, SU)
            pe.wait_ge(const_made, 1)
            pe.wait_ge(dve_setup, 1)
            pe.wait_ge(params_ready, 1)

            def product(dst, pairs):
                ops = [(w, m) for (wh, wl), (mh, ml) in pairs for w, m in ((wh, mh), (wh, ml), (wl, mh))]
                for i, (w, m) in enumerate(ops):
                    last = mm(dst, w, m, start=i == 0, stop=i == len(ops) - 1)
                return last

            def W(i):
                return w_hi[:, i, :], w_lo[:, i, :]

            def transposes(dst, src):
                for b in range(G):
                    last = nc.tensor.transpose(dst[:, b * P:(b + 1) * P], src[:, b], ident[:, :])
                return last

            def step(t, q):
                l, p = t - 1, t + 1
                hT = hT_hi[:, :], hT_lo[:, :]
                h2T = h2_hi[:, :], h2_lo[:, :]

                if has(l):
                    groups(pe, xn2_made, l)
                    groups(pe, cand_made, l - 1)
                    transposes(ps6, xn2).then_inc(h2T_full, 1)
                if has(p):
                    groups(pe, xn1_made, p)
                    groups(pe, z_tanh_made, l - 1)
                    groups(pe, v_made, p - 1)
                    transposes(ps7, xn1).then_inc(hT_full, 1)

                def scores(u):
                    if not has(t):
                        return
                    count(pe, edge_added, t * G + 2 * u)
                    groups(pe, qk_split[3], t)
                    groups(pe, mask_made, t)
                    for r in range(RT):
                        mm(ps_s[:, r, :], ident_bf[:, :],
                           neg[:, 2 * u:2 * u + 2, :].unsqueeze(2).broadcast_to([P, 2, 2, P]),
                           start=True, stop=True)
                    for gg in range(2):
                        for half in range(2):
                            for part, K in enumerate((K_hi, K_lo)):
                                for r in range(RT):
                                    rows = slice(32 * r, 32 * r + 32)
                                    col = 256 * gg + 128 * half
                                    last = mm(ps_s[:, r, col:col + P], Q[rows, q, half, 2 * u + gg, :],
                                              K[rows, q, half, 2 * u + gg, :], start=False,
                                              stop=True, skip_group_check=True)
                    last.then_inc(scores_full, 1)

                def project(n):
                    if not has(p):
                        return
                    if n == 0:
                        groups(pe, hT_lo_made, p)
                    else:
                        groups(pe, qk_split[n - 1], p)
                    product(ps7[:, :], [((qk_hi[:, n // 2, n % 2], qk_lo[:, n // 2, n % 2]), hT)]
                            ).then_inc(qk_full[n], 1)

                scores(0)
                if has(l):
                    groups(pe, h2_lo_made, l)
                    product(ps6[:, :], [(W(W_C1), h2T)]).then_inc(conv1_full, 1)
                project(0)
                if has(l):
                    groups(pe, h1_made, l)
                    product(ps6[:, :], [(W(W_S), h2T)]).then_inc(s_full, 1)
                project(1)
                if has(l):
                    groups(pe, uv_made, l)
                    for b in range(G):
                        sl = slice(b * P, (b + 1) * P)
                        mm(ps6[:, sl], ones2[:, :], msg_bias[:, :], start=True, stop=False)
                        for i, (hh, ww) in enumerate(((h2_hi, w_hi), (h2_hi, w_lo), (h2_lo, w_hi))):
                            last = mm(ps6[:, sl], hh[:, sl], ww[:, W_MSG, :], start=False, stop=i == 2)
                    last.then_inc(msg_full, 1)
                project(2)
                if has(l):
                    groups(pe, msg_made, l)
                    for b in range(G):
                        last = mm(ps6[:, b * P:(b + 1) * P], U[:, b], V[:, b], start=True, stop=True)
                    last.then_inc(dist_full, 1)
                project(3)
                scores(1)
                if has(l):
                    groups(pe, near_made, l)
                    transposes(ps6, adj_t[:, 1 - q]).then_inc(adjT_full, 1)
                if has(p):
                    groups(pe, qk_split[3], p)
                    for b in range(G):
                        sl = slice(b * P, (b + 1) * P)
                        last = product(ps7[:, sl], [((hT_hi[:, sl], hT_lo[:, sl]), W(W_V))])
                    last.then_inc(v_full, 1)

                def taps(first, last_):
                    if not has(l):
                        return
                    if first == 0:
                        groups(pe, AT_made, l)
                        groups(pe, h1_lo_made, l)
                    for tap in range(first, last_):
                        for i, (w, m) in enumerate(((w_hi, h1_hi), (w_hi, h1_lo), (w_lo, h1_hi))):
                            last = mm(ps6[:, :], w[:, W_TAP + tap, :], m[:, :, tap:tap + P],
                                      start=tap + i == 0, stop=tap == TAPS - 1 and i == 2)
                    if last_ == TAPS:
                        last.then_inc(conv2_full, 1)

                def flip(b):
                    if not has(t):
                        return
                    count(pe, exp_made, t * G + (b + 1))
                    for k in range(2):
                        count(pe, probT_made, t * (2 * G) + (2 * b + k - 1))
                        for i in range(4):
                            last = nc.tensor.transpose(ps_t[:, k, i * P:(i + 1) * P], prob[:, b, 4 * k + i],
                                                       ident[:, :])
                        last.then_inc(probT_full, 1)

                def weigh(b):
                    if not has(t):
                        return
                    groups(pe, v_made, t)
                    count(pe, probT_made, t * (2 * G) + (2 * b + 2))
                    if b == 0:
                        groups(pe, n_lo_made, l)
                    if b == 2:
                        count(pe, attn_made, t * 2 + 1)
                    for hp in range(H):
                        h = hp // 2 + RT * (hp % 2)
                        at = (b % 2 * H + h) * (HD + 1)
                        last = mm(ps7[:, at:at + HD + 1], probT[:, b % 2, hp], v_aug[:, q, b, h, :],
                                  start=True, stop=True)
                    last.then_inc(av_full, 1)

                taps(0, 2)
                if has(t - 2):
                    groups(pe, oT_made, t - 2)
                    groups(pe, v_made, p)
                    transposes(ps7, oT).then_inc(outT_full, 1)
                taps(2, 3)
                if has(l):
                    groups(pe, out_made, t - 2)
                    groups(pe, v_made, p)
                    for b in range(G):
                        last = mm(ps7[:, b * P:(b + 1) * P], msg[:, b], AT[:, b], start=True, stop=True)
                    last.then_inc(nmp_full, 1)
                taps(3, 5)
                flip(0)
                taps(5, 7)
                weigh(0)
                flip(1)
                taps(7, 9)
                weigh(1)
                taps(9, 11)
                flip(2)
                taps(11, 13)
                weigh(2)
                flip(3)
                taps(13, 17)
                weigh(3)
                if has(l):
                    groups(pe, attn_made, t, 2)
                    groups(pe, n_lo_made, l)
                    product(ps7[:, :], [(W(W_HN), h2T)]).then_inc(ghn_full, 1)
                if has(t):
                    groups(pe, attn_made, t, 2)
                    groups(pe, y_made, l)
                    transposes(ps6, attn).then_inc(attnT_full, 1)

                def gate(dst, wi0, wi1, wh):
                    pairs = [(W(wh), h2T)] if wh is not None else []
                    pairs += [(W(wi1), (n_hi[:, :], n_lo[:, :])), (W(wi0), (c_hi[:, :], c_lo[:, :]))]
                    return product(dst[:, :], pairs)

                if has(l):
                    groups(pe, ghn_made, l)
                    groups(pe, c_lo_made, l)
                    gate(ps7, W_IR0, W_IR1, W_HR).then_inc(r_full, 1)
                if has(t):
                    groups(pe, aT_lo_made, t)
                    for b in range(G):
                        sl = slice(b * P, (b + 1) * P)
                        last = product(ps6[:, sl], [((aT_hi[:, sl], aT_lo[:, sl]), W(W_O))])
                    last.then_inc(wo_full, 1)
                if has(l):
                    groups(pe, r_tanh_made, l)
                    gate(ps7, W_IZ0, W_IZ1, W_HZ).then_inc(z_full, 1)
                    groups(pe, x2_made, t)
                    gate(ps6, W_IN0, W_IN1, None).then_inc(gin_full, 1)

            run(pe, step)


_INS = ['x', 'adj', 'L0_gnn_W_q', 'L0_gnn_W_k', 'L0_gnn_W_v', 'L0_gnn_W_e', 'L0_gnn_W_o', 'L1_gnn_w_se',
        'L1_gnn_b_se', 'L1_gnn_conv1_w', 'L1_gnn_bn1_g', 'L1_gnn_bn1_b', 'L1_gnn_bn1_m', 'L1_gnn_bn1_v',
        'L1_gnn_conv2_w', 'L1_gnn_bn2_g', 'L1_gnn_bn2_b', 'L1_gnn_bn2_m', 'L1_gnn_bn2_v', 'L1_gnn_w_msg',
        'L1_gnn_b_msg', 'L1_gnn_w_ih', 'L1_gnn_b_ih', 'L1_gnn_w_hh', 'L1_gnn_b_hh']
_OUTS = [((64, 128, 128), 'float32')]


def kernel(**inputs):
    import numpy as _np
    import concourse.bacc as _bacc
    from concourse import mybir as _mybir
    from concourse.bass_utils import run_bass_kernel_spmd as _run

    nc = _bacc.Bacc("TRN2", target_bir_lowering=False, num_devices=1)
    arrays, args = {}, []
    for name in _INS:
        a = _np.ascontiguousarray(inputs[name])
        arrays[f"in_{name}_dram"] = a
        args.append(nc.dram_tensor(f"in_{name}_dram", a.shape, _mybir.dt.from_np(a.dtype), kind="ExternalInput").ap())
    for i, (shape, dtype) in enumerate(_OUTS):
        dt = _mybir.dt.from_np(_np.dtype(dtype))
        args.append(nc.dram_tensor(f"out_{i}_dram", shape, dt, kind="ExternalOutput").ap())
    build(nc, *args)
    r = _run(nc, [arrays], core_ids=[0])
    got = tuple(r.results[0][f"out_{i}_dram"] for i in range(len(_OUTS)))
    return got[0]
```

```python
from contextlib import ExitStack

import concourse.bass as bass
from concourse import mybir

F32 = mybir.dt.float32
F32R = mybir.dt.float32r
BF16 = mybir.dt.bfloat16
ALU = mybir.AluOpType
ACT = mybir.ActivationFunctionType
AX_X = mybir.AxisListType.X

P = 128
H = 8
HD = P // H
RT = 4
G = 4
TAPS = 17
HALO = TAPS // 2
PADDED = P + 2 * HALO
EPS = 1e-5
MASKED = -(2.0 ** 100)

(W_V, W_O, W_C1, W_MSG, W_IR0, W_IR1, W_IZ0, W_IZ1, W_IN0, W_IN1, W_S, W_HR, W_HZ, W_HN,
 W_TAP) = range(15)
BLOCKS = W_TAP + TAPS
(V_G1, V_B1, V_M1, V_V1, V_G2, V_B2, V_M2, V_V2, V_IH, V_HH) = (0, 1, 2, 3, 4, 5, 6, 7, 8, 11)


def build(nc, x, adj, W_q, W_k, W_v, W_e, W_o, w_se, b_se, conv1_w, bn1_g, bn1_b, bn1_m, bn1_v,
          conv2_w, bn2_g, bn2_b, bn2_m, bn2_v, w_msg, b_msg, w_ih, b_ih, w_hh, b_hh, out):
    NG = x.shape[0] // G
    x_g = x.rearrange("(t b) n d -> t n b d", b=G)
    adj_g = adj.rearrange("(t b) n m -> t n b m", b=G)
    out_g = out.rearrange("(t b) n d -> t n b d", b=G)

    ctx = ExitStack()
    with ctx:
        def sb(name, shape, dt=F32):
            return ctx.enter_context(nc.sbuf_tensor(name, shape, dt))

        def sem(name):
            return ctx.enter_context(nc.semaphore(name))

        ident = sb("ident", [P, P])
        ident_bf = sb("ident_bf", [P, P], BF16)
        low_rows = sb("low_rows", [P, 1])
        eps_t = sb("eps_t", [P, G])
        minus_half = sb("minus_half", [P, G])
        ones2 = sb("ones2", [P, P], F32R)
        wq_n, wk_n, wv_n, wo_n = (sb(f"w{c}_n", [P, P]) for c in "qkvo")
        c1_n = sb("c1_n", [P, P])
        msg_n = sb("msg_n", [P, P])
        ih_n = sb("ih_n", [P, 3, 2 * P])
        hh_n = sb("hh_n", [P, 3, P])
        se_n = sb("se_n", [P, P])
        c2_n = sb("c2_n", [P, P, TAPS])
        vec_n = sb("vec_n", [P, P])
        w_hi = sb("w_hi", [P, BLOCKS, P], F32R)
        w_lo = sb("w_lo", [P, BLOCKS, P], F32R)
        qk_hi = sb("qk_hi", [P, 2, 2, P], F32R)
        qk_lo = sb("qk_lo", [P, 2, 2, P], F32R)
        msg_bias = sb("msg_bias", [P, P], F32R)
        bias_n = sb("bias_n", [P, P])
        bias_r = sb("bias_r", [P, P], F32R)
        vec = sb("vec", [P, 16])
        iv = sb("iv", [P, 2])
        scale12 = sb("scale12", [P, 2])
        ms = sb("ms", [P, 2])
        shift12 = sb("shift12", [P, 2])
        rz_sum = sb("rz_sum", [P, 2])
        rz_bias = sb("rz_bias", [P, 2])
        we = sb("we", [P, H])
        we_n = sb("we_n", [P, H])
        se_bias = sb("se_bias", [P, 1])
        fence = sb("fence", [P, 1])
        xt = sb("xt", [P, 2, G, P])
        xn1 = sb("xn1", [P, G, P])
        st1 = sb("st1", [P, G, 6])
        mv1 = sb("mv1", [P, G, 2])
        ve1 = sb("ve1", [P, G])
        rstd1 = sb("rstd1", [P, G])
        hT_hi = sb("hT_hi", [P, G * P], F32R)
        hT_lo = sb("hT_lo", [P, G * P], F32R)
        q_round = sb("q_round", [P, 2, G * P], F32R)
        Q = sb("Q", [P, 2, 2, G, P], F32R)
        K_hi = sb("K_hi", [P, 2, 2, G, P], F32R)
        K_lo = sb("K_lo", [P, 2, 2, G, P], F32R)
        v_aug = sb("v_aug", [P, 2, G, H, HD + 1])
        adj_t = sb("adj_t", [P, 2, G, P])
        neg = sb("neg", [P, G, P], BF16)
        prob = sb("prob", [P, G, H, P])
        smax = sb("smax", [P, G, H])
        probT = sb("probT", [P, 2, H, P])
        rden = sb("rden", [P, 2 * H])
        attn = sb("attn", [P, G, P])
        aT_hi = sb("aT_hi", [P, G * P], F32R)
        aT_lo = sb("aT_lo", [P, G * P], F32R)
        xr = sb("xr", [P, G, P])
        x2 = sb("x2", [P, 2, G, P])
        xn2 = sb("xn2", [P, G, P])
        st2 = sb("st2", [P, G, 6])
        mv2 = sb("mv2", [P, G, 2])
        ve2 = sb("ve2", [P, G])
        rstd2 = sb("rstd2", [P, G])
        h2_hi = sb("h2_hi", [P, G * P], F32R)
        h2_lo = sb("h2_lo", [P, G * P], F32R)
        h2 = sb("h2", [P, G * P])
        res = sb("res", [P, G * P])
        h1 = sb("h1", [P, G, P])
        h1_hi = sb("h1_hi", [P, G, PADDED], F32R)
        h1_lo = sb("h1_lo", [P, G, PADDED], F32R)
        U = sb("U", [P, G, P])
        V = sb("V", [P, G, P])
        msg = sb("msg", [P, G, P])
        near = sb("near", [P, G * P])
        AT = sb("AT", [P, G, P])
        y = sb("y", [P, G * P])
        c_hi = sb("c_hi", [P, G * P], F32R)
        c_lo = sb("c_lo", [P, G * P], F32R)
        n_hi = sb("n_hi", [P, G * P], F32R)
        n_lo = sb("n_lo", [P, G * P], F32R)
        rz = sb("rz", [P, 2, G * P])
        ghn = sb("ghn", [P, G * P])
        rg = sb("rg", [P, G * P])
        cand = sb("cand", [P, G * P])
        nn = sb("nn", [P, G * P])
        hn = sb("hn", [P, G * P])
        oT = sb("oT", [P, G, P])
        out_t = sb("out_t", [P, 2, G, P])

        ps_s = ctx.enter_context(nc.psum_tensor("ps_s", [P, RT, 512], F32))
        ps_t = ctx.enter_context(nc.psum_tensor("ps_t", [P, 2, 512], F32))
        ps6 = ctx.enter_context(nc.psum_tensor("ps6", [P, 512], F32))
        ps7 = ctx.enter_context(nc.psum_tensor("ps7", [P, 512], F32))
        ps_hT, ps_h2T = ps_t[:, 0, :], ps_t[:, 1, :]
        ps_qk = ps6[:, :], ps_t[:, 0, :], ps_t[:, 1, :], ps_t[:, 0, :]
        ps_conv1, ps_s3, ps_msg, ps_dist = ps7[:, :], ps6[:, :], ps7[:, :], ps_t[:, 1, :]
        ps_outT, ps_adjT, ps_v, ps_conv2 = ps6[:, :], ps7[:, :], ps_t[:, 0, :], ps6[:, :]
        ps_nmp, ps_ghn, ps_attnT, ps_wo = ps7[:, :], ps_s[:, 2, :], ps_s[:, 3, :], ps_s[:, 0, :]
        ps_av = ps_s[:, 0, :], ps_s[:, 1, :]
        ps_r, ps_z, ps_gin = ps_s[:, 1, :], ps7[:, :], ps6[:, :]

        ld_vec, ld_qk, ld_w1, ld_w2, ld_c2 = (sem(f"ld_{n}") for n in ("vec", "qk", "w1", "w2", "c2"))
        x_in = [sem("x_in0"), sem("x_in1")]
        adj_in = [sem("adj_in0"), sem("adj_in1")]
        xr_in, v_rows, out_st = sem("xr_in"), sem("v_rows"), [sem("out_st0"), sem("out_st1")]
        const_made, ident_made, zeros_made = sem("const_made"), sem("ident_made"), sem("zeros_made")
        dve_setup, su_full, su_hi, su_done = sem("dve_setup"), sem("su_full"), sem("su_hi"), sem("su_done")
        iv_ready, params_ready = sem("iv_ready"), sem("params_ready")
        iv_sum = sem("iv_sum")
        (h2T_full, hT_full, conv1_full, s_full, msg_full, dist_full, adjT_full, v_full, conv2_full,
         outT_full, nmp_full, av_full, ghn_full, attnT_full, r_full, wo_full, z_full, gin_full,
         scores_full, probT_full) = (sem(n + "_full") for n in (
             "h2T", "hT", "conv1", "s", "msg", "dist", "adjT", "v", "conv2", "outT", "nmp", "av",
             "ghn", "attnT", "r", "wo", "z", "gin", "scores", "probT"))
        qk_full = [sem(f"{n}_full") for n in ("q0", "q1", "k0", "k1")]
        (h2_hi_made, hT_hi_made, h1_made, u_made, msg_made, near_made, v_made, exp_made,
         probT_made, n_hi_made, c_hi_made, ghn_made, aT_hi_made, r_tanh_made, z_tanh_made,
         nn_made) = (sem(n + "_made") for n in (
             "h2_hi", "hT_hi", "h1", "u", "msg", "near", "v", "exp", "probT", "n_hi", "c_hi",
             "ghn", "aT_hi", "r_tanh", "z_tanh", "nn"))
        qk_round = [sem(f"{n}_round") for n in ("q0", "q1", "k0", "k1")]
        (out_made, h2_lo_made, hT_lo_made, edge_added, max_made, shifted, mask_made, AT_made,
         rden_made, attn_made, n_lo_made, y_made, c_lo_made, aT_lo_made, x2_made, r_made, z_made,
         cand_made, xn1_made, xn2_made, stats1, moments1, stats2, moments2) = (
             sem(n) for n in (
                 "out_made", "h2_lo_made", "hT_lo_made", "edge_added", "max_made", "shifted",
                 "mask_made", "AT_made", "rden_made", "attn_made", "n_lo_made", "y_made",
                 "c_lo_made", "aT_lo_made", "x2_made", "r_made", "z_made", "cand_made",
                 "xn1_made", "xn2_made", "stats1", "moments1", "stats2", "moments2"))
        qk_split = [sem(f"{n}_split") for n in ("q0", "q1", "k0", "k1")]
        (edge_made, h2_made, res_made, h1_lo_made, var1_made, rstd1_made, var2_made, rstd2_made,
         rg_made, hn_made, zhn_made, oT_made) = (sem(n) for n in (
             "edge_made", "h2_made", "res_made", "h1_lo_made", "var1_made", "rstd1_made",
             "var2_made", "rstd2_made", "rg_made", "hn_made", "zhn_made", "oT_made"))

        def groups(eng, s, g, each=1):
            if isinstance(g, int):
                g = min(g, NG - 1)
                if g < 0:
                    return
            eng.wait_ge(s, g * each + each)

        def count(eng, s, n):
            if not isinstance(n, int) or n > 0:
                eng.wait_ge(s, n)

        def landed(eng, pair, g, parity):
            eng.wait_ge(pair[parity], (g - parity) * 8 + 16)

        def has(g):
            return not isinstance(g, int) or 0 <= g < NG

        def run(eng, step):
            for t in range(-2, 2):
                step(t, t % 2)
            with eng.Fori(0, (NG - 4) // 2) as i:
                step(2 * i + 2, 0)
                step(2 * i + 3, 1)
            for t in range(NG - 2, NG + 2):
                step(t, t % 2)

        block_src = {W_V: wv_n[:, :], W_O: wo_n[:, :], W_C1: c1_n[:, :], W_MSG: msg_n[:, :],
                     W_S: se_n[:, :], W_HR: hh_n[:, 0, :], W_HZ: hh_n[:, 1, :], W_HN: hh_n[:, 2, :]}
        for gate, first in enumerate((W_IR0, W_IZ0, W_IN0)):
            for part in range(2):
                block_src[first + part] = ih_n[:, gate, part * P:(part + 1) * P]
        for tap in range(TAPS):
            block_src[W_TAP + tap] = c2_n[:, :, tap]
        batches = [range(b, min(b + 4, BLOCKS)) for b in range(0, BLOCKS, 4)]
        LD_VEC = 19
        SU = 3 + len(batches)

        block = ctx.enter_context(nc.Block())

        @block.sync
        def _(sp):
            sp.dma_start(xt[:, 0], x_g[0]).then_inc(x_in[0], 16)
            sp.dma_start(wq_n[:, :], W_q).then_inc(ld_qk, 16)
            sp.dma_start(wk_n[:, :], W_k).then_inc(ld_qk, 16)
            sp.wait_ge(zeros_made, 1)
            for row, v in ((V_G1, bn1_g), (V_B1, bn1_b), (V_M1, bn1_m), (V_V1, bn1_v),
                           (V_G2, bn2_g), (V_B2, bn2_b), (V_M2, bn2_m), (V_V2, bn2_v)):
                sp.dma_start(vec_n[row:row + 1, :], v.unsqueeze(0)).then_inc(ld_vec, 16)
            for row, v in ((V_IH, b_ih), (V_HH, b_hh)):
                sp.dma_start(vec_n[row:row + 3, :], v.rearrange("(g o) -> g o", o=P)).then_inc(ld_vec, 16)
            for row in (0, 32, 64):
                sp.dma_start(se_n[row:row + 3, :], w_se).then_inc(ld_vec, 16)
                sp.dma_start(se_bias[row:row + 3, :], b_se.unsqueeze(1)).then_inc(ld_vec, 16)
            for row in (0, 32):
                sp.dma_start(bias_n[row:row + 1, :], b_msg.unsqueeze(0)).then_inc(ld_vec, 16)
            sp.dma_start(we_n[:, :], W_e.rearrange("h o -> o h").to_broadcast([P, H])).then_inc(ld_vec, 16)
            sp.dma_start(adj_t[:, 0], adj_g[0]).then_inc(adj_in[0], 16)
            for n, w in ((wv_n[:, :], W_v), (wo_n[:, :], W_o),
                         (c1_n[:, :], conv1_w.rearrange("o i k -> o (i k)")), (msg_n[:, :], w_msg)):
                sp.dma_start(n, w).then_inc(ld_w1, 16)
            sp.dma_start(xt[:, 1], x_g[1]).then_inc(x_in[1], 16)
            sp.dma_start(ih_n[:, :, :], w_ih.rearrange("(g o) c -> o g c", o=P)).then_inc(ld_w2, 16)
            sp.dma_start(hh_n[:, :, :], w_hh.rearrange("(g o) c -> o g c", o=P)).then_inc(ld_w2, 16)
            sp.dma_start(c2_n[:, :, :], conv2_w).then_inc(ld_c2, 16)

            def step(t, q):
                if has(t) and has(t + 2):
                    groups(sp, xn1_made, t)
                    sp.dma_start(xt[:, q], x_g[t + 2]).then_inc(x_in[q], 16)
                if has(t - 1):
                    groups(sp, u_made, t - 1)
                    sp.dma_start(V[0:3, :, :], U[0:3, :, :]).then_inc(v_rows, 16)
                    sp.dma_start(V[64:67, :, :], U[32:35, :, :]).then_inc(v_rows, 16)
                if has(t):
                    groups(sp, x2_made, t - 1)
                    sp.dma_start(xr[:, :, :], x_g[t]).then_inc(xr_in, 16)
                if has(t - 2):
                    groups(sp, out_made, t - 2)
                    sp.dma_start(out_g[t - 2], out_t[:, q]).then_inc(out_st[q], 16)
                if has(t + 1) and not (isinstance(t, int) and t == -1):
                    groups(sp, adjT_full, t - 1)
                    groups(sp, mask_made, t - 1)
                    groups(sp, edge_made, t - 1, G)
                    sp.dma_start(adj_t[:, 1 - q], adj_g[t + 1]).then_inc(adj_in[1 - q], 16)

            run(sp, step)
            for q in range(2):
                sp.wait_ge(out_st[q], 16 * (NG // 2))

        @block.gpsimd
        def _(gp):
            gp.memset(ident[:, :], 0.0).then_inc(ident_made, 1)
            gp.memset(vec_n[:, :], 0.0)
            gp.memset(se_n[:, :], 0.0)
            gp.memset(se_bias[:, :], 0.0)
            gp.memset(bias_n[:, :], 0.0).then_inc(zeros_made, 1)
            gp.wait_ge(ident_made, 1)
            gp.affine_select(out=ident[:, :], in_=ident[:, :], compare_op=ALU.not_equal, fill=1.0,
                             base=0, pattern=[[-1, P]], channel_multiplier=1).then_inc(ident_made, 1)
            gp.memset(eps_t[:, :], EPS)
            gp.memset(minus_half[:, :], -0.5)
            gp.memset(v_aug[:, :, :, :, :].rearrange("p a b c d -> p (a b c d)"), 1.0)
            gp.memset(U[:, :, :], 0.0)
            gp.memset(V[:, :, :], 0.0)
            gp.memset(h1_hi[:, :, :].bitcast(F32), 0.0)
            gp.memset(h1_lo[:, :, :].bitcast(F32), 0.0)
            gp.memset(msg_bias[:, :].bitcast(F32), 0.0)
            gp.memset(ones2[:, :].bitcast(F32), 0.0).then_inc(ident_made, 1)
            gp.wait_ge(ident_made, 3)
            gp.memset(U[64:67, :, :], -0.5)
            gp.memset(V[32:35, :, :], -0.5)
            gp.memset(ones2[0:1, :].bitcast(F32), 1.0)
            gp.memset(ones2[32:33, :].bitcast(F32), 1.0).then_inc(const_made, 1)
            gp.wait_ge(const_made, 1)

            def rstd(mv, ve, out_, moments, var_made, made, g):
                groups(gp, moments, g)
                gp.tensor_tensor(ve[:, :], mv[:, :, 1], eps_t[:, :], ALU.add).then_inc(var_made, 1)
                groups(gp, var_made, g)
                gp.tensor_tensor(out_[:, :], ve[:, :], minus_half[:, :], ALU.pow).then_inc(made, 1)

            def edge(g, b, parity):
                gp.tensor_tensor(prob[:, b], adj_t[:, parity, b].unsqueeze(1).broadcast_to([P, H, P]),
                                 we[:, :].unsqueeze(2).broadcast_to([P, H, P]), ALU.mult
                                 ).then_inc(edge_made, 1)

            def step(t, q):
                l = t - 1
                if has(l):
                    groups(gp, h2_lo_made, l)
                    gp.tensor_tensor(h2[:, :], h2_hi[:, :].bitcast(F32), h2_lo[:, :].bitcast(F32),
                                     ALU.add).then_inc(h2_made, 1)
                    groups(gp, h2_made, l)
                    groups(gp, y_made, l - 1)
                    gp.tensor_tensor(res[:, :], h2[:, :], shift12[:, 1:2].to_broadcast([P, G * P]),
                                     ALU.add).then_inc(res_made, 1)
                    groups(gp, h1_made, l)
                    groups(gp, conv2_full, l - 1)
                    gp.tensor_tensor(h1_lo[:, :, HALO:HALO + P], h1[:, :, :],
                                     h1_hi[:, :, HALO:HALO + P].bitcast(F32), ALU.subtract
                                     ).then_inc(h1_lo_made, 1)
                if isinstance(t, int) and t == -2:
                    rstd(mv1, ve1, rstd1, moments1, var1_made, rstd1_made, 0)
                    return
                if has(t + 1):
                    landed(gp, adj_in, t + 1, 1 - q)
                    for b in range(G):
                        count(gp, probT_full, t * (2 * G) + (2 * b + 2) if has(t) else 0)
                        edge(t + 1, b, 1 - q)
                        if b == 1 and has(t + 2):
                            rstd(mv1, ve1, rstd1, moments1, var1_made, rstd1_made, t + 2)
                elif has(t + 2):
                    rstd(mv1, ve1, rstd1, moments1, var1_made, rstd1_made, t + 2)
                if has(t):
                    rstd(mv2, ve2, rstd2, moments2, var2_made, rstd2_made, t)
                if has(l):
                    groups(gp, ghn_made, l)
                    groups(gp, r_made, l)
                    groups(gp, cand_made, l - 1)
                    gp.tensor_tensor(rg[:, :], ghn[:, :], rz[:, 0], ALU.mult).then_inc(rg_made, 1)
                    groups(gp, nn_made, l)
                    gp.tensor_tensor(hn[:, :], h2[:, :], nn[:, :], ALU.subtract).then_inc(hn_made, 1)
                    groups(gp, hn_made, l)
                    groups(gp, z_made, l)
                    gp.tensor_tensor(hn[:, :], hn[:, :], rz[:, 1], ALU.mult).then_inc(zhn_made, 1)
                    groups(gp, zhn_made, l)
                    groups(gp, outT_full, l - 1)
                    gp.tensor_tensor(oT[:, :, :].rearrange("p b n -> p (b n)"), hn[:, :], nn[:, :],
                                     ALU.add).then_inc(oT_made, 1)

            gp.wait_ge(su_hi, 3)
            gp.tensor_tensor(iv[:, :], vec[:, V_V1:V_V2 + 1:4], eps_t[:, 0:2], ALU.add).then_inc(iv_sum, 1)
            gp.wait_ge(iv_sum, 1)
            gp.tensor_tensor(iv[:, :], iv[:, :], minus_half[:, 0:2], ALU.pow).then_inc(iv_ready, 1)
            gp.wait_ge(params_ready, 1)
            run(gp, step)

        @block.scalar
        def _(act):
            for n in range(SU):
                act.wait_ge(su_full, n + 1)
                src = ps_t[:, n % 2, :]
                if n < 2:
                    for rep in range(2):
                        dst = qk_hi[:, n].rearrange("p f (r s d) -> p (f r) s d", s=2, d=HD)[:, :, rep]
                        last = nc.scalar.activation(dst, src[:, 0:P].rearrange("p (a d) -> p a d", d=HD),
                                                    ACT.Copy, scale=0.25 if n == 0 else 1.0)
                    last.then_inc(su_hi, 1)
                elif n == 2:
                    nc.scalar.activation(vec[:, :], src[:, 0:16], ACT.Copy).then_inc(su_hi, 1)
                else:
                    bl = batches[n - 3]
                    nc.scalar.activation(w_hi[:, bl[0]:bl[-1] + 1, :].rearrange("p a b -> p (a b)"),
                                         src[:, 0:len(bl) * P], ACT.Copy).then_inc(su_hi, 1)
            act.wait_ge(params_ready, 1)
            act.wait_ge(const_made, 1)

            def step(t, q):
                l, p = t - 1, t + 1
                if has(p):
                    groups(act, hT_full, p)
                    groups(act, v_full, p - 1)
                    nc.scalar.activation(hT_hi[:, :], ps_hT, ACT.Relu).then_inc(hT_hi_made, 1)
                if has(l):
                    groups(act, h2T_full, l)
                    groups(act, z_full, l - 1)
                    groups(act, h2_made, l - 1)
                    nc.scalar.activation(h2_hi[:, :], ps_h2T, ACT.Relu).then_inc(h2_hi_made, 1)

                def round_qk(n):
                    if not has(p):
                        return
                    groups(act, qk_full[n], p)
                    if n < 2:
                        groups(act, qk_split[n], p - 1)
                        dst = q_round[:, n]
                    else:
                        groups(act, scores_full, p - 2, 2)
                        dst = K_hi[:, 1 - q, n - 2].rearrange("p b n -> p (b n)")
                    nc.scalar.activation(dst, ps_qk[n], ACT.Copy).then_inc(qk_round[n], 1)

                def exp(b):
                    if not has(t):
                        return
                    count(act, shifted, t * G + b + 1)
                    e = prob[:, b].rearrange("p h n -> p (h n)")
                    nc.scalar.activation(e, e, ACT.Exp).then_inc(exp_made, 1)

                def copy_probT(b):
                    if not has(t):
                        return
                    count(act, av_full, t * G + (b - 1))
                    for k in range(2):
                        count(act, probT_full, t * (2 * G) + (2 * b + k + 1))
                        nc.scalar.activation(probT[:, b % 2, 4 * k:4 * k + 4].rearrange("p h n -> p (h n)"),
                                             ps_t[:, k, :], ACT.Copy).then_inc(probT_made, 1)

                round_qk(0)
                round_qk(1)
                if has(l):
                    groups(act, conv1_full, l)
                    groups(act, h1_lo_made, l - 1)
                    groups(act, conv2_full, l - 1)
                    nc.scalar.activation(h1[:, :, :].rearrange("p b n -> p (b n)"), ps_conv1, ACT.Relu,
                                         bias=shift12[:, 0:1], scale=scale12[:, 0:1])
                    nc.scalar.activation(h1_hi[:, :, HALO:HALO + P], ps_conv1.rearrange("p (b n) -> p b n", b=G),
                                         ACT.Relu, bias=shift12[:, 0:1], scale=scale12[:, 0:1]
                                         ).then_inc(h1_made, 1)
                round_qk(2)
                if has(l):
                    groups(act, s_full, l)
                    groups(act, dist_full, l - 1)
                    count(act, v_rows, 32 * l)
                    for row, f in ((0, ACT.Identity), (32, ACT.Square)):
                        last = nc.scalar.activation(U[row:row + 3, :, :].rearrange("p b n -> p (b n)"),
                                                    ps_s3[row:row + 3, :], f, bias=se_bias[row:row + 3, :])
                    last.then_inc(u_made, 1)
                round_qk(3)
                exp(0)
                if has(l):
                    groups(act, msg_full, l)
                    groups(act, nmp_full, l - 1)
                    nc.scalar.activation(msg[:, :, :].rearrange("p b n -> p (b n)"), ps_msg, ACT.Relu
                                         ).then_inc(msg_made, 1)
                    groups(act, dist_full, l)
                    groups(act, AT_made, l - 1)
                    nc.scalar.activation(near[:, :], ps_dist, ACT.Exp, scale=2.0).then_inc(near_made, 1)
                exp(1)
                if has(p):
                    groups(act, v_full, p)
                    groups(act, av_full, p - 2, G)
                    nc.scalar.activation(v_aug[:, 1 - q, :, :, 0:HD].rearrange("p b h d -> p (b h) d"),
                                         ps_v.rearrange("p (a d) -> p a d", d=HD), ACT.Copy
                                         ).then_inc(v_made, 1)
                copy_probT(0)
                if has(l):
                    groups(act, nmp_full, l)
                    groups(act, gin_full, l - 1)
                    nc.scalar.activation(n_hi[:, :], ps_nmp, ACT.Copy).then_inc(n_hi_made, 1)
                copy_probT(1)
                exp(2)
                copy_probT(2)
                exp(3)
                copy_probT(3)
                if has(t):
                    groups(act, attnT_full, t)
                    groups(act, wo_full, t - 1)
                    nc.scalar.activation(aT_hi[:, :], ps_attnT, ACT.Copy).then_inc(aT_hi_made, 1)
                if has(l):
                    groups(act, y_made, l)
                    groups(act, gin_full, l - 1)
                    nc.scalar.activation(c_hi[:, :], y[:, :], ACT.Relu).then_inc(c_hi_made, 1)
                    groups(act, ghn_full, l)
                    groups(act, rg_made, l - 1)
                    nc.scalar.activation(ghn[:, :], ps_ghn, ACT.Identity,
                                         bias=vec[:, V_HH + 2:V_HH + 3]).then_inc(ghn_made, 1)
                    groups(act, oT_made, l - 1)
                    groups(act, r_full, l)
                    nc.scalar.activation(rz[:, 0], ps_r, ACT.Tanh, bias=rz_bias[:, 0:1], scale=0.5
                                         ).then_inc(r_tanh_made, 1)
                    groups(act, z_full, l)
                    nc.scalar.activation(rz[:, 1], ps_z, ACT.Tanh, bias=rz_bias[:, 1:2], scale=0.5
                                         ).then_inc(z_tanh_made, 1)
                    groups(act, cand_made, l)
                    nc.scalar.activation(nn[:, :], cand[:, :], ACT.Tanh, bias=vec[:, V_IH + 2:V_IH + 3]
                                         ).then_inc(nn_made, 1)

            run(act, step)

        @block.vector
        def _(dve):
            V_ = nc.vector
            dve.wait_ge(ident_made, 2)
            V_.tensor_copy(ident_bf[:, :], ident[:, :])
            V_.tensor_reduce(
                low_rows[:, :], ident[:, :].rearrange("p (r s d) -> p r s d", s=2, d=HD)[:, :, 1],
                mybir.AxisListType.XY, ALU.add, negate=True).then_inc(dve_setup, 1)
            for n in range(SU):
                dve.wait_ge(su_hi, n + 1)
                src = ps_t[:, n % 2, :]
                if n < 2:
                    for rep in range(2):
                        hi = qk_hi[:, n].rearrange("p f (r s d) -> p (f r) s d", s=2, d=HD)[:, :, rep]
                        lo = qk_lo[:, n].rearrange("p f (r s d) -> p (f r) s d", s=2, d=HD)[:, :, rep]
                        last = V_.scalar_tensor_tensor(lo, src[:, 0:P].rearrange("p (a d) -> p a d", d=HD),
                                                       0.25 if n == 0 else 1.0, hi.bitcast(F32),
                                                       ALU.mult, ALU.subtract)
                    last.then_inc(su_done, 1)
                elif n == 2:
                    dve.wait_ge(iv_ready, 1)
                    V_.tensor_tensor(rz_sum[:, :], vec[:, V_IH:V_IH + 2], vec[:, V_HH:V_HH + 2], ALU.add)
                    V_.tensor_tensor(scale12[:, :], vec[:, V_G1:V_G2 + 1:4], iv[:, :], ALU.mult).then_inc(dve_setup, 1)
                    dve.wait_ge(dve_setup, 2)
                    V_.tensor_scalar(rz_bias[:, :], rz_sum[:, :], 0.5, None, ALU.mult)
                    V_.tensor_tensor(ms[:, :], vec[:, V_M1:V_M2 + 1:4], scale12[:, :], ALU.mult).then_inc(dve_setup, 1)
                    dve.wait_ge(ld_vec, 16 * LD_VEC)
                    dve.wait_ge(const_made, 1)
                    V_.tensor_copy(we[:, :].rearrange("p (r f) -> p r f", f=2),
                                   we_n[:, :].rearrange("p (f r) -> p r f", f=2))
                    V_.tensor_copy(msg_bias[0:1, :], bias_n[0:1, :])
                    V_.tensor_copy(bias_r[32:33, :], bias_n[32:33, :]).then_inc(dve_setup, 1)
                    dve.wait_ge(dve_setup, 4)
                    V_.tensor_tensor(msg_bias[32:33, :], bias_n[32:33, :], bias_r[32:33, :].bitcast(F32), ALU.subtract)
                    V_.tensor_tensor(shift12[:, :], vec[:, V_B1:V_B2 + 1:4], ms[:, :], ALU.subtract
                                     ).then_inc(params_ready, 1)
                    V_.memset(fence[:, :], 0.0).then_inc(su_done, 1)
                else:
                    bl = batches[n - 3]
                    hi, lo = (w[:, bl[0]:bl[-1] + 1, :].rearrange("p a b -> p (a b)") for w in (w_hi, w_lo))
                    V_.tensor_tensor(lo, src[:, 0:len(bl) * P], hi.bitcast(F32), ALU.subtract).then_inc(su_done, 1)

            def moments(src, st, mv, stats, made, g):
                for b in range(G):
                    V_.bn_stats(st[:, b], src[:, b]).then_inc(stats, 1)
                groups(dve, stats, g, G)
                V_.memset(fence[:, :], 0.0)
                for b in range(G):
                    last = V_.bn_aggr(mv[:, b], st[:, b])
                last.then_inc(made, 1)

            def normalise(dst, src, mv, rs, made):
                for b in range(G):
                    last = V_.tensor_scalar(dst[:, b], src[:, b], mv[:, b, 0:1], rs[:, b:b + 1],
                                            ALU.subtract, ALU.mult)
                last.then_inc(made, 1)

            def layernorm1(g, parity):
                landed(dve, x_in, g, parity)
                groups(dve, rstd1_made, g - 1)
                moments(xt[:, parity], st1, mv1, stats1, moments1, g)
                groups(dve, rstd1_made, g)
                groups(dve, hT_full, g - 1)
                normalise(xn1, xt[:, parity], mv1, rstd1, xn1_made)

            def mask(g, parity):
                landed(dve, adj_in, g, parity)
                V_.tensor_scalar(neg[:, :, :], adj_t[:, parity], 0.0, MASKED, ALU.is_equal, ALU.mult
                                 ).then_inc(mask_made, 1)

            def step(t, q):
                l, p = t - 1, t + 1
                first = isinstance(t, int) and t == -2
                if first:
                    layernorm1(0, 0)
                    return
                def add_edge(b):
                    if has(t):
                        count(dve, scores_full, t * 2 + (b // 2 + 1))
                        count(dve, edge_made, t * G + (b + 1))
                        e = prob[:, b].rearrange("p (r f) n -> p r (f n)", f=2)
                        V_.tensor_tensor(e, ps_s[:, :, 256 * (b % 2):256 * (b % 2) + 256], e, ALU.add
                                         ).then_inc(edge_added, 1)

                def split_qk(n):
                    if not has(p):
                        return
                    groups(dve, qk_round[n], p)
                    groups(dve, scores_full, p - 2, 2)
                    if n < 2:
                        V_.scalar_tensor_tensor(Q[:, 1 - q, n].rearrange("p b n -> p (b n)"),
                                                q_round[:, n].bitcast(F32), low_rows[:, 0:1], ps_qk[n],
                                                ALU.mult, ALU.add).then_inc(qk_split[n], 1)
                    else:
                        hi, lo = (K[:, 1 - q, n - 2].rearrange("p b n -> p (b n)") for K in (K_hi, K_lo))
                        V_.tensor_tensor(lo, ps_qk[n], hi.bitcast(F32), ALU.subtract
                                         ).then_inc(qk_split[n], 1)

                def row_max(b):
                    if has(t):
                        count(dve, edge_added, t * G + (b + 1))
                        V_.reduce_max(smax[:, b], prob[:, b], AX_X).then_inc(max_made, 1)

                def shift(b):
                    if has(t):
                        count(dve, max_made, t * G + (b + 1))
                        V_.tensor_tensor(prob[:, b], prob[:, b], smax[:, b].unsqueeze(2).broadcast_to([P, H, P]),
                                         ALU.subtract).then_inc(shifted, 1)

                def norm_attn(u):
                    if not has(t):
                        return
                    count(dve, av_full, t * G + (2 * u + 2))
                    av = ps_av[u][:, 0:2 * H * (HD + 1)].rearrange("p (a d) -> p a d", d=HD + 1)
                    count(dve, attn_made, t * 2 + u)
                    V_.reciprocal(rden[:, :], av[:, :, HD]).then_inc(rden_made, 1)
                    count(dve, rden_made, t * 2 + (u + 1))
                    groups(dve, attnT_full, t - 1)
                    V_.tensor_tensor(attn[:, 2 * u:2 * u + 2].rearrange("p b (h d) -> p (b h) d", d=HD),
                                     av[:, :, 0:HD], rden[:, :].unsqueeze(2).broadcast_to([P, 2 * H, HD]),
                                     ALU.mult).then_inc(attn_made, 1)

                if has(p):
                    groups(dve, hT_hi_made, p)
                    groups(dve, v_full, p - 1)
                    V_.scalar_tensor_tensor(hT_lo[:, :], ps_hT, 0.0, hT_hi[:, :].bitcast(F32),
                                            ALU.max, ALU.subtract).then_inc(hT_lo_made, 1)
                add_edge(0)
                if has(l):
                    groups(dve, h2_hi_made, l)
                    groups(dve, z_full, l - 1)
                    groups(dve, h2_made, l - 1)
                    V_.scalar_tensor_tensor(h2_lo[:, :], ps_h2T, 0.0, h2_hi[:, :].bitcast(F32),
                                            ALU.max, ALU.subtract).then_inc(h2_lo_made, 1)
                add_edge(1)
                split_qk(0)
                split_qk(1)
                row_max(0)
                shift(0)
                split_qk(2)
                row_max(1)
                split_qk(3)
                shift(1)
                if has(t - 2):
                    groups(dve, outT_full, t - 2)
                    count(dve, out_st[q], (t - 2 - q) * 8)
                    V_.tensor_tensor(out_t[:, q].rearrange("p b n -> p (b n)"), ps_outT,
                                     x2[:, q].rearrange("p b n -> p (b n)"), ALU.add).then_inc(out_made, 1)
                add_edge(2)
                add_edge(3)
                if has(l):
                    groups(dve, near_made, l)
                    groups(dve, adjT_full, l)
                    groups(dve, nmp_full, l - 1)
                    V_.tensor_tensor(AT[:, :, :].rearrange("p b n -> p (b n)"), ps_adjT, near[:, :],
                                     ALU.mult).then_inc(AT_made, 1)
                row_max(2)
                shift(2)
                if has(l):
                    groups(dve, n_hi_made, l)
                    groups(dve, gin_full, l - 1)
                    V_.tensor_tensor(n_lo[:, :], ps_nmp, n_hi[:, :].bitcast(F32), ALU.subtract
                                     ).then_inc(n_lo_made, 1)
                row_max(3)
                shift(3)
                norm_attn(0)
                if has(p):
                    groups(dve, scores_full, t, 2)
                    mask(p, 1 - q)
                if has(t + 2):
                    layernorm1(t + 2, q)
                norm_attn(1)
                if has(l):
                    groups(dve, conv2_full, l)
                    groups(dve, res_made, l)
                    groups(dve, c_hi_made, l - 1)
                    V_.scalar_tensor_tensor(y[:, :], ps_conv2, scale12[:, 1:2], res[:, :], ALU.mult, ALU.add
                                            ).then_inc(y_made, 1)
                if has(t):
                    groups(dve, aT_hi_made, t)
                    groups(dve, wo_full, t - 1)
                    V_.tensor_tensor(aT_lo[:, :], ps_attnT, aT_hi[:, :].bitcast(F32), ALU.subtract
                                     ).then_inc(aT_lo_made, 1)
                if has(l):
                    groups(dve, c_hi_made, l)
                    groups(dve, gin_full, l - 1)
                    V_.scalar_tensor_tensor(c_lo[:, :], y[:, :], 0.0, c_hi[:, :].bitcast(F32),
                                            ALU.max, ALU.subtract).then_inc(c_lo_made, 1)
                if has(t):
                    groups(dve, wo_full, t)
                    dve.wait_ge(xr_in, t * 16 + 16)
                    V_.tensor_tensor(x2[:, q].rearrange("p b n -> p (b n)"), ps_wo,
                                     xr[:, :, :].rearrange("p b n -> p (b n)"), ALU.add).then_inc(x2_made, 1)
                    groups(dve, x2_made, t)
                    moments(x2[:, q], st2, mv2, stats2, moments2, t)
                if has(l):
                    groups(dve, r_tanh_made, l)
                    V_.tensor_scalar(rz[:, 0], rz[:, 0], 0.5, 0.5, ALU.mult, ALU.add).then_inc(r_made, 1)
                if has(t):
                    groups(dve, rstd2_made, t)
                    groups(dve, h2T_full, t - 1)
                    normalise(xn2, x2[:, q], mv2, rstd2, xn2_made)
                if has(l):
                    groups(dve, z_tanh_made, l)
                    V_.tensor_scalar(rz[:, 1], rz[:, 1], 0.5, 0.5, ALU.mult, ALU.add).then_inc(z_made, 1)
                    groups(dve, rg_made, l)
                    groups(dve, gin_full, l)
                    groups(dve, nn_made, l - 1)
                    V_.tensor_tensor(cand[:, :], ps_gin, rg[:, :], ALU.add).then_inc(cand_made, 1)

            run(dve, step)

        @block.tensor
        def _(pe):
            mm = nc.tensor.matmul

            pe.wait_ge(ident_made, 2)
            for n in range(SU):
                if n >= 2:
                    pe.wait_ge(su_done, n - 1)
                if n == 0:
                    pe.wait_ge(ld_qk, 32)
                if n == 2:
                    pe.wait_ge(ld_vec, 16 * LD_VEC)
                if n == 3:
                    pe.wait_ge(ld_w1, 64)
                if n == 4:
                    pe.wait_ge(ld_w2, 32)
                if n >= 3 and W_TAP in batches[n - 3]:
                    pe.wait_ge(ld_c2, 16)
                src = {0: [wq_n[:, :]], 1: [wk_n[:, :]], 2: [vec_n[:, :]]}.get(n) or [
                    block_src[i] for i in batches[n - 3]]
                for i, w in enumerate(src):
                    last = nc.tensor.transpose(ps_t[:, n % 2, i * P:(i + 1) * P], w, ident[:, :])
                last.then_inc(su_full, 1)
            pe.wait_ge(su_done, SU)
            pe.wait_ge(const_made, 1)
            pe.wait_ge(dve_setup, 1)
            pe.wait_ge(params_ready, 1)

            def product(dst, pairs):
                ops = [(w, m) for (wh, wl), (mh, ml) in pairs for w, m in ((wh, mh), (wh, ml), (wl, mh))]
                for i, (w, m) in enumerate(ops):
                    last = mm(dst, w, m, start=i == 0, stop=i == len(ops) - 1)
                return last

            def W(i):
                return w_hi[:, i, :], w_lo[:, i, :]

            def transposes(dst, src):
                for b in range(G):
                    last = nc.tensor.transpose(dst[:, b * P:(b + 1) * P], src[:, b], ident[:, :])
                return last

            def step(t, q):
                l, p = t - 1, t + 1
                hT = hT_hi[:, :], hT_lo[:, :]
                h2T = h2_hi[:, :], h2_lo[:, :]

                def scores(u):
                    if not has(t):
                        return
                    count(pe, edge_added, t * G + 2 * u)
                    if u == 0:
                        groups(pe, ghn_made, l - 1)
                        groups(pe, aT_lo_made, t - 1)
                        groups(pe, x2_made, t - 1)
                        groups(pe, r_tanh_made, l - 1)
                    groups(pe, qk_split[3], t)
                    groups(pe, mask_made, t)
                    for r in range(RT):
                        mm(ps_s[:, r, :], ident_bf[:, :],
                           neg[:, 2 * u:2 * u + 2, :].unsqueeze(2).broadcast_to([P, 2, 2, P]),
                           start=True, stop=True)
                    for gg in range(2):
                        for half in range(2):
                            for part, K in enumerate((K_hi, K_lo)):
                                for r in range(RT):
                                    rows = slice(32 * r, 32 * r + 32)
                                    col = 256 * gg + 128 * half
                                    last = mm(ps_s[:, r, col:col + P], Q[rows, q, half, 2 * u + gg, :],
                                              K[rows, q, half, 2 * u + gg, :], start=False,
                                              stop=True, skip_group_check=True)
                    last.then_inc(scores_full, 1)

                def project(n):
                    if not has(p):
                        return
                    if n == 0:
                        groups(pe, cand_made, l - 1)
                    if n == 1:
                        groups(pe, hT_lo_made, p)
                    if n == 2:
                        groups(pe, h2_lo_made, l)
                    if n == 3:
                        groups(pe, qk_split[1], p)
                    groups(pe, hT_lo_made, p)
                    product(ps_qk[n], [((qk_hi[:, n // 2, n % 2], qk_lo[:, n // 2, n % 2]), hT)]
                            ).then_inc(qk_full[n], 1)

                def taps(first, last_):
                    if not has(l):
                        return
                    if first == 0:
                        groups(pe, out_made, t - 2)
                        groups(pe, u_made, l)
                        groups(pe, h1_lo_made, l)
                    for tap in range(first, last_):
                        for i, (w, m) in enumerate(((w_hi, h1_hi), (w_hi, h1_lo), (w_lo, h1_hi))):
                            last = mm(ps_conv2, w[:, W_TAP + tap, :], m[:, :, tap:tap + P],
                                      start=tap + i == 0, stop=tap == TAPS - 1 and i == 2)
                    if last_ == TAPS:
                        last.then_inc(conv2_full, 1)

                def flip(b):
                    if not has(t):
                        return
                    if b == 0:
                        groups(pe, v_made, p)
                        groups(pe, near_made, l)
                        groups(pe, qk_split[2], p)
                    count(pe, exp_made, t * G + (b + 1))
                    for k in range(2):
                        count(pe, probT_made, t * (2 * G) + (2 * b + k - 1))
                        for i in range(4):
                            last = nc.tensor.transpose(ps_t[:, k, i * P:(i + 1) * P], prob[:, b, 4 * k + i],
                                                       ident[:, :])
                        last.then_inc(probT_full, 1)

                def weigh(b):
                    if not has(t):
                        return
                    groups(pe, v_made, t)
                    count(pe, probT_made, t * (2 * G) + (2 * b + 2))
                    count(pe, edge_added, t * G + G)
                    for hp in range(H):
                        h = hp // 2 + RT * (hp % 2)
                        at = (b % 2 * H + h) * (HD + 1)
                        last = mm(ps_av[b // 2][:, at:at + HD + 1], probT[:, b % 2, hp], v_aug[:, q, b, h, :],
                                  start=True, stop=True)
                    last.then_inc(av_full, 1)

                def gate(dst, wi0, wi1, wh):
                    ops = [(W(wh), h2T)] if wh is not None else []
                    ops += [(W(wi1), (n_hi[:, :], n_lo[:, :])), (W(wi0), (c_hi[:, :], c_lo[:, :]))]
                    for k, ((wh_, wl_), (mh, ml)) in enumerate(ops):
                        if k == len(ops) - 1:
                            groups(pe, c_lo_made, l)
                        for i, (w, m) in enumerate(((wh_, mh), (wh_, ml), (wl_, mh))):
                            last = mm(dst, w, m, start=k + i == 0, stop=k == len(ops) - 1 and i == 2)
                    return last

                if has(p):
                    groups(pe, xn1_made, p)
                    count(pe, probT_made, t * (2 * G))
                    groups(pe, v_made, p - 1)
                    transposes(ps_hT, xn1).then_inc(hT_full, 1)
                scores(0)
                if has(l):
                    groups(pe, xn2_made, l)
                    groups(pe, probT_made, t - 1, 2 * G)
                    transposes(ps_h2T, xn2).then_inc(h2T_full, 1)
                project(0)
                project(1)
                if has(l):
                    groups(pe, h2_lo_made, l)
                    groups(pe, z_tanh_made, l - 1)
                    product(ps_conv1, [(W(W_C1), h2T)]).then_inc(conv1_full, 1)
                project(2)
                if has(l):
                    groups(pe, qk_split[0], p)
                    groups(pe, cand_made, l - 1)
                    product(ps_s3, [(W(W_S), h2T)]).then_inc(s_full, 1)
                project(3)
                if has(l):
                    groups(pe, h1_made, l)
                    for b in range(G):
                        sl = slice(b * P, (b + 1) * P)
                        mm(ps_msg[:, sl], ones2[:, :], msg_bias[:, :], start=True, stop=False)
                        for i, (hh, ww) in enumerate(((h2_hi, w_hi), (h2_hi, w_lo), (h2_lo, w_hi))):
                            last = mm(ps_msg[:, sl], hh[:, sl], ww[:, W_MSG, :], start=False, stop=i == 2)
                    last.then_inc(msg_full, 1)
                if has(t - 2):
                    groups(pe, oT_made, t - 2)
                    groups(pe, u_made, l)
                    groups(pe, cand_made, t - 2)
                    transposes(ps_outT, oT).then_inc(outT_full, 1)
                scores(1)
                if has(l):
                    count(pe, v_rows, l * 32 + 32)
                    groups(pe, qk_split[2], p)
                    for b in range(G):
                        last = mm(ps_dist[:, b * P:(b + 1) * P], U[:, b], V[:, b], start=True, stop=True)
                    last.then_inc(dist_full, 1)
                if has(p):
                    groups(pe, qk_split[3], p)
                    for b in range(G):
                        sl = slice(b * P, (b + 1) * P)
                        last = product(ps_v[:, sl], [((hT_hi[:, sl], hT_lo[:, sl]), W(W_V))])
                    last.then_inc(v_full, 1)
                if has(l):
                    groups(pe, msg_made, l)
                    transposes(ps_adjT, adj_t[:, 1 - q]).then_inc(adjT_full, 1)
                taps(0, 2)
                flip(0)
                taps(2, 4)
                flip(1)
                if has(l):
                    groups(pe, AT_made, l)
                    for b in range(G):
                        last = mm(ps_nmp[:, b * P:(b + 1) * P], msg[:, b], AT[:, b], start=True, stop=True)
                    last.then_inc(nmp_full, 1)
                weigh(0)
                taps(4, 6)
                weigh(1)
                taps(6, 9)
                flip(2)
                taps(9, 12)
                flip(3)
                weigh(2)
                taps(12, 14)
                weigh(3)
                taps(14, 17)
                if has(t):
                    groups(pe, attn_made, t, 2)
                    count(pe, edge_added, t * G + G)
                    transposes(ps_attnT, attn).then_inc(attnT_full, 1)
                if has(l):
                    groups(pe, edge_added, t, G)
                    groups(pe, ghn_made, l - 1)
                    product(ps_ghn, [(W(W_HN), h2T)]).then_inc(ghn_full, 1)
                    groups(pe, attn_made, t, 2)
                    groups(pe, r_tanh_made, l - 1)
                    groups(pe, n_lo_made, l)
                    gate(ps_r, W_IR0, W_IR1, W_HR).then_inc(r_full, 1)
                if has(t):
                    groups(pe, aT_lo_made, t)
                    groups(pe, attn_made, t, 2)
                    for b in range(G):
                        sl = slice(b * P, (b + 1) * P)
                        last = product(ps_wo[:, sl], [((aT_hi[:, sl], aT_lo[:, sl]), W(W_O))])
                    last.then_inc(wo_full, 1)
                if has(l):
                    groups(pe, n_lo_made, l)
                    gate(ps_z, W_IZ0, W_IZ1, W_HZ).then_inc(z_full, 1)
                    groups(pe, y_made, l)
                    gate(ps_gin, W_IN0, W_IN1, None).then_inc(gin_full, 1)

            run(pe, step)


_INS = ['x', 'adj', 'L0_gnn_W_q', 'L0_gnn_W_k', 'L0_gnn_W_v', 'L0_gnn_W_e', 'L0_gnn_W_o', 'L1_gnn_w_se',
        'L1_gnn_b_se', 'L1_gnn_conv1_w', 'L1_gnn_bn1_g', 'L1_gnn_bn1_b', 'L1_gnn_bn1_m', 'L1_gnn_bn1_v',
        'L1_gnn_conv2_w', 'L1_gnn_bn2_g', 'L1_gnn_bn2_b', 'L1_gnn_bn2_m', 'L1_gnn_bn2_v', 'L1_gnn_w_msg',
        'L1_gnn_b_msg', 'L1_gnn_w_ih', 'L1_gnn_b_ih', 'L1_gnn_w_hh', 'L1_gnn_b_hh']
_OUTS = [((64, 128, 128), 'float32')]


def kernel(**inputs):
    import numpy as _np
    import concourse.bacc as _bacc
    from concourse import mybir as _mybir
    from concourse.bass_utils import run_bass_kernel_spmd as _run

    nc = _bacc.Bacc("TRN2", target_bir_lowering=False, num_devices=1)
    arrays, args = {}, []
    for name in _INS:
        a = _np.ascontiguousarray(inputs[name])
        arrays[f"in_{name}_dram"] = a
        args.append(nc.dram_tensor(f"in_{name}_dram", a.shape, _mybir.dt.from_np(a.dtype), kind="ExternalInput").ap())
    for i, (shape, dtype) in enumerate(_OUTS):
        dt = _mybir.dt.from_np(_np.dtype(dtype))
        args.append(nc.dram_tensor(f"out_{i}_dram", shape, dt, kind="ExternalOutput").ap())
    build(nc, *args)
    r = _run(nc, [arrays], core_ids=[0])
    got = tuple(r.results[0][f"out_{i}_dram"] for i in range(len(_OUTS)))
    return got[0]
```

```python
from contextlib import ExitStack

import concourse.bass as bass
from concourse import mybir

F32 = mybir.dt.float32
F32R = mybir.dt.float32r
ALU = mybir.AluOpType
ACT = mybir.ActivationFunctionType
AX_X = mybir.AxisListType.X

P = 128
H = 8
HD = P // H
RT = 2
SLOTS = H // RT
G = 4
TAPS = 17
HALO = TAPS // 2
PADDED = P + 2 * HALO + 2
EPS = 1e-5
MASKED = -(2.0 ** 100)

HALF = P // 2
EVEN_TAPS, ODD_TAPS = TAPS // 2 + 1, TAPS // 2

W_V, W_O, W_MSG = range(3)
(W_C1, W_IR0, W_IR1, W_IZ0, W_IZ1, W_IN0, W_IN1, W_S, W_HR, W_HZ, W_HN, W_TAP) = range(12)
W_PAIR = W_TAP + TAPS
BLOCKS = W_PAIR + TAPS // 2
(V_G1, V_B1, V_M1, V_V1, V_G2, V_B2, V_M2, V_V2, V_IH, V_HH) = (0, 1, 2, 3, 4, 5, 6, 7, 8, 11)


def build(nc, x, adj, W_q, W_k, W_v, W_e, W_o, w_se, b_se, conv1_w, bn1_g, bn1_b, bn1_m, bn1_v,
          conv2_w, bn2_g, bn2_b, bn2_m, bn2_v, w_msg, b_msg, w_ih, b_ih, w_hh, b_hh, out):
    NG = x.shape[0] // G
    x_g = x.rearrange("(t b) n d -> t n b d", b=G)
    adj_g = adj.rearrange("(t b) n m -> t n b m", b=G)
    out_g = out.rearrange("(t b) n d -> t n b d", b=G)

    ctx = ExitStack()
    with ctx:
        def sb(name, shape, dt=F32):
            return ctx.enter_context(nc.sbuf_tensor(name, shape, dt))

        def sem(name):
            return ctx.enter_context(nc.semaphore(name))

        ident = sb("ident", [P, P])
        eps_t = sb("eps_t", [P, G])
        minus_half = sb("minus_half", [P, G])
        ones2 = sb("ones2", [P, P], F32R)
        w_hi = sb("w_hi", [P, BLOCKS, P], F32R)
        w_lo = sb("w_lo", [P, BLOCKS, P], F32R)
        w_full = sb("w_full", [P, 3, P])
        qk_hi = sb("qk_hi", [P, 2, HD, H], F32R)
        qk_lo = sb("qk_lo", [P, 2, HD, H], F32R)
        msg_bias = sb("msg_bias", [P, P], F32R)
        bias_r = sb("bias_r", [P, P], F32R)
        vec = sb("vec", [P, 16])
        iv = sb("iv", [P, 2])
        scale12 = sb("scale12", [P, 2])
        minus_scale = sb("minus_scale", [P, 1])
        ms = sb("ms", [P, 2])
        shift12 = sb("shift12", [P, 2])
        rz_sum = sb("rz_sum", [P, 2])
        rz_bias = sb("rz_bias", [P, 2])
        we = sb("we", [P, H])
        se_bias = sb("se_bias", [P, 1])
        fence = sb("fence", [P, 4])
        xt = sb("xt", [P, 2, G, P])
        xn1 = sb("xn1", [P, G, P])
        st1 = sb("st1", [P, G, 6])
        mv1 = sb("mv1", [P, G, 2])
        ve1 = sb("ve1", [P, G])
        rstd1 = sb("rstd1", [P, G])
        hT_hi = sb("hT_hi", [P, G * P], F32R)
        hT_lo = sb("hT_lo", [P, G * P], F32R)
        hT = sb("hT", [P, G * P])
        qk_split = [sb(f"{n}_split", [P, 2, G * P], F32R) for n in "qk"]
        qk_dram = nc.dram_tensor("qk_dram", [2, 2, P, G * P], F32).ap()
        Q = sb("Q", [P, 2, SLOTS, G, P], F32R)
        K = sb("K", [P, 2, SLOTS, G, P], F32R)
        v_pad = sb("v_pad", [P, G, H // 2, 4, HD])
        adj_t = sb("adj_t", [P, 2, G, P])
        neg = sb("neg", [P, G, P])
        prob = sb("prob", [P, G, H, P])
        smax = sb("smax", [P, G, H])
        minus_max = sb("minus_max", [P, G, H])
        sums = sb("sums", [P, G, H])
        probT = sb("probT", [P, 2, H, P])
        rden = sb("rden", [P, G, H])
        aT = sb("aT", [P, G * P])
        xr = sb("xr", [P, G, P])
        x2 = sb("x2", [P, 2, G, P])
        xn2 = sb("xn2", [P, G, P])
        st2 = sb("st2", [P, G, 6])
        mv2 = sb("mv2", [P, G, 2])
        ve2 = sb("ve2", [P, G])
        rstd2 = sb("rstd2", [P, G])
        h2_hi = sb("h2_hi", [P, G * P], F32R)
        h2_lo = sb("h2_lo", [P, G * P], F32R)
        h2 = sb("h2", [P, 2, G * P])
        res = sb("res", [P, G * P])
        h1 = sb("h1", [P, G, P])
        h1_hi = sb("h1_hi", [P, G, PADDED], F32R)
        h1_lo = sb("h1_lo", [P, G, PADDED], F32R)
        pair = sb("pair", [P, G, HALF])
        pair_hi = sb("pair_hi", [P, G, HALF + HALO], F32R)
        pair_lo = sb("pair_lo", [P, G, HALF + HALO], F32R)
        odd = sb("odd", [P, G, HALF + 2])
        odd_sub = sb("odd_sub", [P, G, HALF])
        odd_res = sb("odd_res", [P, G, HALF])
        U = sb("U", [P, G, P])
        V = sb("V", [P, G, P])
        msg = sb("msg", [P, G, P])
        AT = sb("AT", [P, G, P])
        c_hi = sb("c_hi", [P, G * P], F32R)
        c_lo = sb("c_lo", [P, G * P], F32R)
        n_hi = sb("n_hi", [P, G * P], F32R)
        n_lo = sb("n_lo", [P, G * P], F32R)
        ghn = sb("ghn", [P, G * P])
        late = sb("late", [P, 10, G * P])
        rz = late[:, 0:2]
        near, y, rg, cand, nn, one_z, zh, zn = (late[:, i] for i in range(2, 10))
        staged = late[:, :, :].rearrange("p a n -> p (a n)")
        cuts = {}
        at = 0
        for name, size in (("c2", P * TAPS), ("ih", 6 * P), ("hh", 3 * P), ("q", P), ("k", P), ("v", P),
                           ("o", P), ("c1", P), ("msg", P), ("se", P), ("vec", P), ("bias", P)):
            cuts[name] = staged[:, at:at + size]
            at += size
        c2_n = cuts["c2"].rearrange("p (i k) -> p i k", k=TAPS)
        ih_n = cuts["ih"].rearrange("p (g c) -> p g c", g=3)
        hh_n = cuts["hh"].rearrange("p (g c) -> p g c", g=3)
        wq_n, wk_n, wv_n, wo_n, c1_n, msg_n, se_n, vec_n, bias_n = (
            cuts[name] for name in ("q", "k", "v", "o", "c1", "msg", "se", "vec", "bias"))
        oT = sb("oT", [P, G, P])
        out_t = sb("out_t", [P, 2, G, P])

        ps_s = ctx.enter_context(nc.psum_tensor("ps_s", [P, 4, 512], F32))
        ps_t = ctx.enter_context(nc.psum_tensor("ps_t", [P, 2, 512], F32))
        ps6 = ctx.enter_context(nc.psum_tensor("ps6", [P, 512], F32))
        ps7 = ctx.enter_context(nc.psum_tensor("ps7", [P, 512], F32))
        bank = [ps_s[:, i, :] for i in range(4)] + [ps_t[:, 0, :], ps_t[:, 1, :], ps6[:, :], ps7[:, :]]
        ps_av = bank[0]
        ps_scores = ps_t[:, 0:2, :], ps_s[:, 2:4, :], ps_s[:, 0:2, :], ps_s[:, 2:4, :]
        ps_hT, ps_ghn = bank[0], bank[2]
        ps_outT, ps_wo = bank[3], bank[3]
        ps_qk = bank[1], bank[0]
        ps_adjT, ps_s3, ps_v = bank[4], bank[4], bank[5]
        ps_r, ps_gin = bank[0], bank[1]
        ps_h2T, ps_msg = bank[6], bank[6]
        ps_even, ps_pairs = (bank[6][:, 0:G * HALF].rearrange("p (b m) -> p b m", b=G),) * 2
        ps_odd = bank[7][:, 0:G * (HALF + 2)].rearrange("p (b m) -> p b m", b=G)
        ps_conv1, ps_dist, ps_nmp, ps_z = (bank[7],) * 4

        ld_vec, ld_qk, ld_we, ld_w1, ld_w2, ld_c2 = (
            sem(f"ld_{n}") for n in ("vec", "qk", "we", "w1", "w2", "c2"))
        qk_out = [sem("q_out"), sem("k_out")]
        qk_stacked = sem("qk_stacked")
        x_in = [sem("x_in0"), sem("x_in1")]
        adj_in = [sem("adj_in0"), sem("adj_in1")]
        xr_in, v_rows, out_st = sem("xr_in"), sem("v_rows"), [sem("out_st0"), sem("out_st1")]
        const_made, ident_made, zeros_made = sem("const_made"), sem("ident_made"), sem("zeros_made")
        dve_setup, su_full, su_hi, su_done = sem("dve_setup"), sem("su_full"), sem("su_hi"), sem("su_done")
        iv_ready, params_ready = sem("iv_ready"), sem("params_ready")
        iv_sum = sem("iv_sum")
        (h2T_full, hT_full, conv1_full, s_full, msg_full, dist_full, adjT_full, v_full, conv2_full,
         outT_full, nmp_full, av_full, ghn_full, r_full, wo_full, z_full, gin_full,
         scores_full, probT_full) = (sem(n + "_full") for n in (
             "h2T", "hT", "conv1", "s", "msg", "dist", "adjT", "v", "conv2", "outT", "nmp", "av",
             "ghn", "r", "wo", "z", "gin", "scores", "probT"))
        qk_full = [sem(f"{n}_full") for n in ("q", "k")]
        odd_full, even_full = sem("odd_full"), sem("even_full")
        (h2_made, hT_made, h1_made, u_made, msg_made, near_made, v_made, exp_made,
         probT_made, n_hi_made, c_hi_made, ghn_made, aT_made, r_tanh_made, z_tanh_made,
         nn_made) = (sem(n + "_made") for n in (
             "h2", "hT", "h1", "u", "msg", "near", "v", "exp", "probT", "n_hi", "c_hi",
             "ghn", "aT", "r_tanh", "z_tanh", "nn"))
        adjT_made, pair_hi_made, odd_made = sem("adjT_made"), sem("pair_hi_made"), sem("odd_made")
        qk_hi_made = [sem(f"{n}_hi_made") for n in ("q", "k")]
        (out_made, h2_lo_made, hT_lo_made, edge_added, max_made, max_negated, mask_made, AT_made,
         rden_made, scaled, n_lo_made, y_made, c_lo_made, x2_made, r_made, z_made,
         cand_made, xn1_made, xn2_made, stats1, moments1, stats2, moments2) = (
             sem(n) for n in (
                 "out_made", "h2_lo_made", "hT_lo_made", "edge_added", "max_made", "max_negated",
                 "mask_made", "AT_made", "rden_made", "scaled", "n_lo_made", "y_made",
                 "c_lo_made", "x2_made", "r_made", "z_made", "cand_made",
                 "xn1_made", "xn2_made", "stats1", "moments1", "stats2", "moments2"))
        qk_lo_made = [sem(f"{n}_lo_made") for n in ("q", "k")]
        odd_added, odd_res_made = sem("odd_added"), sem("odd_res_made")
        (edge_scaled, edge_made, res_made, h1_lo_made, var1_made, rstd1_made, var2_made, rstd2_made,
         rg_made, zh_made, zn_made, oT_made) = (sem(n) for n in (
             "edge_scaled", "edge_made", "res_made", "h1_lo_made", "var1_made", "rstd1_made",
             "var2_made", "rstd2_made", "rg_made", "zh_made", "zn_made", "oT_made"))
        pair_made, pair_lo_made = sem("pair_made"), sem("pair_lo_made")

        def groups(eng, s, g, each=1):
            if isinstance(g, int):
                g = min(g, NG - 1)
                if g < 0:
                    return
            eng.wait_ge(s, g * each + each)

        def count(eng, s, n):
            if not isinstance(n, int) or n > 0:
                eng.wait_ge(s, n)

        def landed(eng, pair, g, parity):
            eng.wait_ge(pair[parity], (g - parity) * 8 + 16)

        def by_feature(src):
            return src[:, 0:P].rearrange("p (h d) -> p d h", h=H)

        def has(g):
            return not isinstance(g, int) or 0 <= g < NG

        def run(eng, step):
            for t in range(-2, 2):
                step(t, t % 2)
            with eng.Fori(0, (NG - 4) // 2) as i:
                step(2 * i + 2, 0)
                step(2 * i + 3, 1)
            for t in range(NG - 2, NG + 2):
                step(t, t % 2)

        pair_src = {W_PAIR + k - 1: (c2_n[:, :, 2 * k - 1], c2_n[:, :, 2 * k]) for k in range(1, EVEN_TAPS)}
        block_src = {W_C1: c1_n, W_S: se_n, W_HR: hh_n[:, 0, :], W_HZ: hh_n[:, 1, :], W_HN: hh_n[:, 2, :]}
        for gate, first in enumerate((W_IR0, W_IZ0, W_IN0)):
            for part in range(2):
                block_src[first + part] = ih_n[:, gate, part * P:(part + 1) * P]
        for tap in range(TAPS):
            block_src[W_TAP + tap] = c2_n[:, :, tap]
        batches = [range(b, min(b + 4, BLOCKS)) for b in range(0, BLOCKS, 4)]
        LD_VEC = 15
        SU = 4 + len(batches)

        block = ctx.enter_context(nc.Block())

        @block.sync
        def _(sp):
            sp.dma_start(xt[:, 0], x_g[0]).then_inc(x_in[0], 16)
            sp.dma_start(wq_n, W_q).then_inc(ld_qk, 16)
            sp.dma_start(wk_n, W_k).then_inc(ld_qk, 16)
            sp.dma_start(adj_t[:, 0], adj_g[0]).then_inc(adj_in[0], 16)
            sp.dma_start(we[:, :], W_e.rearrange("h o -> o h").to_broadcast([P, H])).then_inc(ld_we, 16)
            for n, w in ((wv_n, W_v), (wo_n, W_o), (c1_n, conv1_w.rearrange("o i k -> o (i k)")),
                         (msg_n, w_msg)):
                sp.dma_start(n, w).then_inc(ld_w1, 16)
            sp.dma_start(xt[:, 1], x_g[1]).then_inc(x_in[1], 16)
            sp.wait_ge(zeros_made, 1)
            sp.dma_start(ih_n, w_ih.rearrange("(g o) c -> o g c", o=P)).then_inc(ld_w2, 16)
            sp.dma_start(hh_n, w_hh.rearrange("(g o) c -> o g c", o=P)).then_inc(ld_w2, 16)
            for row in (0, 32, 64):
                sp.dma_start(se_n[row:row + 3, :], w_se).then_inc(ld_w2, 16)
            sp.dma_start(c2_n, conv2_w).then_inc(ld_c2, 16)
            for row, v in ((V_G1, bn1_g), (V_B1, bn1_b), (V_M1, bn1_m), (V_V1, bn1_v),
                           (V_G2, bn2_g), (V_B2, bn2_b), (V_M2, bn2_m), (V_V2, bn2_v)):
                sp.dma_start(vec_n[row:row + 1, :], v.unsqueeze(0)).then_inc(ld_vec, 16)
            for row, v in ((V_IH, b_ih), (V_HH, b_hh)):
                sp.dma_start(vec_n[row:row + 3, :], v.rearrange("(g o) -> g o", o=P)).then_inc(ld_vec, 16)
            for row in (0, 32, 64):
                sp.dma_start(se_bias[row:row + 3, :], b_se.unsqueeze(1)).then_inc(ld_vec, 16)
            for row in (0, 32):
                sp.dma_start(bias_n[row:row + 1, :], b_msg.unsqueeze(0)).then_inc(ld_vec, 16)

            def step(t, q):
                if has(t) and has(t + 2):
                    groups(sp, xn1_made, t)
                    sp.dma_start(xt[:, q], x_g[t + 2]).then_inc(x_in[q], 16)
                if has(t):
                    groups(sp, x2_made, t - 1)
                    sp.dma_start(xr[:, :, :], x_g[t]).then_inc(xr_in, 16)
                if has(t + 1) and not (isinstance(t, int) and t == -1):
                    groups(sp, adjT_full, t - 1)
                    groups(sp, mask_made, t - 1)
                    groups(sp, edge_made, t - 1, G)
                    sp.dma_start(adj_t[:, 1 - q], adj_g[t + 1]).then_inc(adj_in[1 - q], 16)
                if has(t + 1):
                    for n in range(2):
                        groups(sp, qk_lo_made[n], t + 1)
                        sp.dma_start(qk_dram[n].rearrange("w c n -> c w n"),
                                     qk_split[n][:, :, :].bitcast(F32)).then_inc(qk_out[n], 16)
                if has(t - 1):
                    groups(sp, u_made, t - 1)
                    sp.dma_start(V[0:3, :, :], U[0:3, :, :]).then_inc(v_rows, 16)
                    sp.dma_start(V[64:67, :, :], U[32:35, :, :]).then_inc(v_rows, 16)
                if has(t + 1):
                    for n, stack in enumerate((Q, K)):
                        sp.wait_ge(qk_out[n], (t + 1) * 16 + 16)
                        if n == 0:
                            groups(sp, scores_full, t - 1, G)
                        for tile in range(RT):
                            src = qk_dram[n].rearrange("w (d t a) n -> t (w d) (a n)", t=RT, a=SLOTS)[tile]
                            for row, at, size in ((0, 0, 2 * HD),) + (
                                    ((2 * HD, 0, 2 * HD),) if n == 0 else ((2 * HD, HD, HD), (3 * HD, 0, HD))):
                                row += 64 * tile
                                sp.dma_start(stack[row:row + size, 1 - q].rearrange("p a b n -> p (a b n)").bitcast(F32),
                                             src[at:at + size]).then_inc(qk_stacked, 16)
                if has(t - 2):
                    groups(sp, out_made, t - 2)
                    sp.dma_start(out_g[t - 2], out_t[:, q]).then_inc(out_st[q], 16)

            run(sp, step)
            for q in range(2):
                sp.wait_ge(out_st[q], 16 * (NG // 2))

        @block.gpsimd
        def _(gp):
            gp.memset(ident[:, :], 0.0).then_inc(ident_made, 1)
            gp.memset(vec_n, 0.0)
            gp.memset(se_n, 0.0)
            gp.memset(se_bias[:, :], 0.0)
            gp.memset(bias_n, 0.0).then_inc(zeros_made, 1)
            gp.wait_ge(ident_made, 1)
            gp.affine_select(out=ident[:, :], in_=ident[:, :], compare_op=ALU.not_equal, fill=1.0,
                             base=0, pattern=[[-1, P]], channel_multiplier=1).then_inc(ident_made, 1)
            gp.memset(eps_t[:, :], EPS)
            gp.memset(minus_half[:, :], -0.5)
            gp.memset(v_pad[:, :, :, :, :].rearrange("p b k f d -> p (b k f d)"), 0.0)
            gp.memset(U[:, :, :], 0.0)
            gp.memset(V[:, :, :], 0.0)
            gp.memset(h1_hi[:, :, :].bitcast(F32), 0.0)
            gp.memset(h1_lo[:, :, :].bitcast(F32), 0.0)
            gp.memset(pair_hi[:, :, :].bitcast(F32), 0.0)
            gp.memset(pair_lo[:, :, :].bitcast(F32), 0.0)
            gp.memset(msg_bias[:, :].bitcast(F32), 0.0)
            gp.memset(ones2[:, :].bitcast(F32), 0.0).then_inc(ident_made, 1)
            gp.wait_ge(ident_made, 3)
            gp.memset(U[64:67, :, :], -0.5)
            gp.memset(V[32:35, :, :], -0.5)
            gp.memset(ones2[0:1, :].bitcast(F32), 1.0)
            gp.memset(ones2[32:33, :].bitcast(F32), 1.0).then_inc(const_made, 1)
            gp.wait_ge(const_made, 1)

            def rstd(mv, ve, out_, moments, var_made, made, g):
                groups(gp, moments, g)
                gp.tensor_tensor(ve[:, :], mv[:, :, 1], eps_t[:, :], ALU.add).then_inc(var_made, 1)
                groups(gp, var_made, g)
                gp.tensor_tensor(out_[:, :], ve[:, :], minus_half[:, :], ALU.pow).then_inc(made, 1)

            def edge(g, b, parity):
                gp.tensor_tensor(prob[:, b], adj_t[:, parity, b].unsqueeze(1).broadcast_to([P, H, P]),
                                 we[:, :].unsqueeze(2).broadcast_to([P, H, P]), ALU.mult
                                 ).then_inc(edge_scaled, 1)
                count(gp, edge_scaled, g * G + (b + 1))
                gp.tensor_tensor(prob[:, b], prob[:, b], neg[:, b].unsqueeze(1).broadcast_to([P, H, P]),
                                 ALU.add).then_inc(edge_made, 1)

            def step(t, q):
                l = t - 1
                if isinstance(t, int) and t == 1:
                    gp.wait_ge(params_ready, 1)
                if has(l):
                    groups(gp, h1_made, l)
                    groups(gp, conv2_full, l - 1)
                    gp.tensor_tensor(h1_lo[:, :, HALO:HALO + P], h1[:, :, :],
                                     h1_hi[:, :, HALO:HALO + P].bitcast(F32), ALU.subtract
                                     ).then_inc(h1_lo_made, 1)
                    groups(gp, pair_lo_made, l - 1)
                    halves = h1[:, :, :].rearrange("p b (m e) -> p b m e", e=2)
                    gp.tensor_tensor(pair[:, :, :], halves[:, :, :, 0], halves[:, :, :, 1], ALU.add
                                     ).then_inc(pair_made, 1)
                if has(l - 1):
                    groups(gp, nn_made, l - 1)
                    gp.tensor_tensor(zn[:, :], one_z[:, :], nn[:, :], ALU.mult).then_inc(zn_made, 1)
                    groups(gp, zn_made, l - 1)
                    groups(gp, outT_full, l - 2)
                    gp.tensor_tensor(oT[:, :, :].rearrange("p b n -> p (b n)"), zh[:, :], zn[:, :],
                                     ALU.add).then_inc(oT_made, 1)
                if has(l):
                    groups(gp, pair_hi_made, l)
                    groups(gp, pair_made, l)
                    gp.tensor_tensor(pair_lo[:, :, HALO // 2:HALO // 2 + HALF], pair[:, :, :],
                                     pair_hi[:, :, HALO // 2:HALO // 2 + HALF].bitcast(F32), ALU.subtract
                                     ).then_inc(pair_lo_made, 1)
                    groups(gp, h2_made, l)
                    groups(gp, y_made, l - 1)
                    gp.tensor_tensor(res[:, :], h2[:, 1 - q], shift12[:, 1:2].to_broadcast([P, G * P]),
                                     ALU.add).then_inc(res_made, 1)
                if isinstance(t, int) and t == -2:
                    rstd(mv1, ve1, rstd1, moments1, var1_made, rstd1_made, 0)
                    return
                if has(t + 1):
                    landed(gp, adj_in, t + 1, 1 - q)
                    groups(gp, mask_made, t + 1)
                    for b in range(G):
                        count(gp, probT_full, t * (2 * G) + (2 * b + 2) if has(t) else 0)
                        edge(t + 1, b, 1 - q)
                        if b == (1 if isinstance(t, int) and t == -1 else 2) and has(t + 2):
                            rstd(mv1, ve1, rstd1, moments1, var1_made, rstd1_made, t + 2)
                        if b == 2 and isinstance(t, int) and t == -1:
                            gp.wait_ge(su_hi, SU)
                            gp.tensor_tensor(iv[:, :], vec[:, V_V1:V_V2 + 1:4], eps_t[:, 0:2], ALU.add
                                             ).then_inc(iv_sum, 1)
                            gp.wait_ge(iv_sum, 1)
                            gp.tensor_tensor(iv[:, :], iv[:, :], minus_half[:, 0:2], ALU.pow
                                             ).then_inc(iv_ready, 1)
                elif has(t + 2):
                    rstd(mv1, ve1, rstd1, moments1, var1_made, rstd1_made, t + 2)
                if has(t):
                    rstd(mv2, ve2, rstd2, moments2, var2_made, rstd2_made, t)
                if has(l):
                    groups(gp, ghn_made, l)
                    groups(gp, r_made, l)
                    groups(gp, cand_made, l - 1)
                    gp.tensor_tensor(rg[:, :], ghn[:, :], rz[:, 0], ALU.mult).then_inc(rg_made, 1)
                    groups(gp, z_made, l)
                    gp.tensor_tensor(zh[:, :], h2[:, 1 - q], rz[:, 1], ALU.mult).then_inc(zh_made, 1)

            gp.wait_ge(ld_we, 16)
            run(gp, step)

        @block.scalar
        def _(act):
            for n in range(2):
                act.wait_ge(su_full, n + 1)
                nc.scalar.activation(qk_hi[:, n], by_feature(ps_t[:, n, :]), ACT.Copy,
                                     scale=HD ** -0.5 if n == 0 else 1.0).then_inc(su_hi, 1)

            def setup():
                act.wait_ge(su_full, 3)
                nc.scalar.activation(w_full[:, :, :].rearrange("p a b -> p (a b)"), ps_t[:, 0, 0:3 * P],
                                     ACT.Copy).then_inc(su_hi, 1)
                for n, bl in enumerate(batches, 3):
                    act.wait_ge(su_full, n + 1)
                    src = ps_t[:, n % 2, :]
                    nc.scalar.activation(w_hi[:, bl[0]:bl[-1] + 1, :].rearrange("p a b -> p (a b)"),
                                         src[:, 0:len(bl) * P], ACT.Copy).then_inc(su_hi, 1)
                act.wait_ge(su_full, SU)
                nc.scalar.activation(vec[:, :], ps_t[:, (SU - 1) % 2, 0:16], ACT.Copy).then_inc(su_hi, 1)
                act.wait_ge(const_made, 1)

            def step(t, q):
                l, p = t - 1, t + 1

                def high_qk(n):
                    if has(p):
                        groups(act, qk_full[n], p)
                        groups(act, qk_out[n], p - 1, 16)
                        nc.scalar.activation(qk_split[n][:, 0], ps_qk[n], ACT.Copy
                                             ).then_inc(qk_hi_made[n], 1)

                def exp(g, b):
                    if not has(g):
                        return
                    count(act, max_negated, g * G + b + 1)
                    for h in range(H):
                        last = nc.scalar.activation(prob[:, b, h], prob[:, b, h], ACT.Exp,
                                                    bias=minus_max[:, b, h:h + 1], accum_out=sums[:, b, h:h + 1])
                    last.then_inc(exp_made, 1)

                def copy_probT(b):
                    if not has(t):
                        return
                    count(act, av_full, t * G + (b - 1))
                    for k in range(2):
                        count(act, probT_full, t * (2 * G) + (2 * b + k + 1))
                        nc.scalar.activation(probT[:, b % 2, 4 * k:4 * k + 4].rearrange("p h n -> p (h n)"),
                                             ps_t[:, k, :], ACT.Copy).then_inc(probT_made, 1)

                if isinstance(t, int) and t == 1:
                    act.wait_ge(params_ready, 1)
                if has(l):
                    groups(act, h2T_full, l)
                    groups(act, z_full, l - 1)
                    nc.scalar.activation(h2_hi[:, :], ps_h2T, ACT.Relu)
                    groups(act, zh_made, l - 2)
                    nc.scalar.activation(h2[:, 1 - q], ps_h2T, ACT.Relu).then_inc(h2_made, 1)
                if has(l):
                    groups(act, adjT_full, l)
                    groups(act, nmp_full, l - 1)
                    nc.scalar.activation(AT[:, :, :].rearrange("p b n -> p (b n)"), ps_adjT, ACT.Copy
                                         ).then_inc(adjT_made, 1)
                if has(p):
                    groups(act, hT_full, p)
                    groups(act, v_full, p - 1)
                    nc.scalar.activation(hT_hi[:, :], ps_hT, ACT.Relu)
                    nc.scalar.activation(hT[:, :], ps_hT, ACT.Relu).then_inc(hT_made, 1)
                if has(l - 1):
                    groups(act, cand_made, l - 1)
                    nc.scalar.activation(nn[:, :], cand[:, :], ACT.Tanh, bias=vec[:, V_IH + 2:V_IH + 3]
                                         ).then_inc(nn_made, 1)
                if has(l):
                    groups(act, conv1_full, l)
                    groups(act, pair_made, l - 1)
                    groups(act, conv2_full, l - 1)
                    nc.scalar.activation(h1[:, :, :].rearrange("p b n -> p (b n)"), ps_conv1, ACT.Relu,
                                         bias=shift12[:, 0:1], scale=scale12[:, 0:1])
                    nc.scalar.activation(h1_hi[:, :, HALO:HALO + P], ps_conv1.rearrange("p (b n) -> p b n", b=G),
                                         ACT.Relu, bias=shift12[:, 0:1], scale=scale12[:, 0:1]
                                         ).then_inc(h1_made, 1)
                high_qk(0)
                high_qk(1)
                if has(t):
                    groups(act, v_full, t)
                    groups(act, av_full, t - 1, G)
                    nc.scalar.activation(v_pad[:, :, :, 0:4:3, :].rearrange("p b k e d -> p (b k) e d"),
                                         ps_v.rearrange("p (k e d) -> p k e d", e=2, d=HD), ACT.Copy
                                         ).then_inc(v_made, 1)
                if has(l):
                    groups(act, msg_full, l)
                    groups(act, nmp_full, l - 1)
                    nc.scalar.activation(msg[:, :, :].rearrange("p b n -> p (b n)"), ps_msg, ACT.Relu
                                         ).then_inc(msg_made, 1)
                if has(l):
                    groups(act, s_full, l)
                    groups(act, dist_full, l - 1)
                    count(act, v_rows, 32 * l)
                    for row, f in ((0, ACT.Identity), (32, ACT.Square)):
                        last = nc.scalar.activation(U[row:row + 3, :, :].rearrange("p b n -> p (b n)"),
                                                    ps_s3[row:row + 3, :], f, bias=se_bias[row:row + 3, :])
                    last.then_inc(u_made, 1)
                if has(l):
                    groups(act, pair_made, l)
                    nc.scalar.activation(pair_hi[:, :, HALO // 2:HALO // 2 + HALF], pair[:, :, :], ACT.Copy
                                         ).then_inc(pair_hi_made, 1)
                exp(t, 1)
                if has(l):
                    groups(act, odd_full, l)
                    groups(act, odd_added, l - 1)
                    nc.scalar.activation(odd[:, :, :], ps_odd, ACT.Copy).then_inc(odd_made, 1)
                copy_probT(0)
                exp(t, 2)
                if has(l):
                    groups(act, dist_full, l)
                    groups(act, AT_made, l - 1)
                    nc.scalar.activation(near[:, :], ps_dist, ACT.Exp, scale=2.0).then_inc(near_made, 1)
                copy_probT(1)
                exp(t, 3)
                copy_probT(2)
                if has(l):
                    groups(act, nmp_full, l)
                    groups(act, gin_full, l - 1)
                    nc.scalar.activation(n_hi[:, :], ps_nmp, ACT.Copy).then_inc(n_hi_made, 1)
                copy_probT(3)
                if has(t):
                    groups(act, av_full, t, G)
                    groups(act, wo_full, t - 1)
                    nc.scalar.activation(aT[:, :], ps_av, ACT.Copy).then_inc(aT_made, 1)
                if has(l):
                    groups(act, y_made, l)
                    groups(act, gin_full, l - 1)
                    nc.scalar.activation(c_hi[:, :], y[:, :], ACT.Relu).then_inc(c_hi_made, 1)
                    groups(act, ghn_full, l)
                    groups(act, rg_made, l - 1)
                    nc.scalar.activation(ghn[:, :], ps_ghn, ACT.Identity,
                                         bias=vec[:, V_HH + 2:V_HH + 3]).then_inc(ghn_made, 1)
                if isinstance(t, int) and t == -1:
                    setup()
                exp(p, 0)
                if has(l):
                    groups(act, oT_made, l - 1)
                    groups(act, r_full, l)
                    nc.scalar.activation(rz[:, 0], ps_r, ACT.Tanh, bias=rz_bias[:, 0:1], scale=0.5
                                         ).then_inc(r_tanh_made, 1)
                    groups(act, z_full, l)
                    nc.scalar.activation(rz[:, 1], ps_z, ACT.Tanh, bias=rz_bias[:, 1:2], scale=0.5
                                         ).then_inc(z_tanh_made, 1)

            run(act, step)

        @block.vector
        def _(dve):
            V_ = nc.vector
            for n in range(2):
                dve.wait_ge(su_hi, n + 1)
                V_.scalar_tensor_tensor(qk_lo[:, n], by_feature(ps_t[:, n, :]), HD ** -0.5 if n == 0 else 1.0,
                                        qk_hi[:, n].bitcast(F32), ALU.mult, ALU.subtract
                                        ).then_inc(su_done, 1)

            def setup():
                dve.wait_ge(su_hi, 3)
                V_.memset(fence[:, 2:3], 0.0).then_inc(su_done, 1)
                for n, bl in enumerate(batches, 3):
                    dve.wait_ge(su_hi, n + 1)
                    hi, lo = (w[:, bl[0]:bl[-1] + 1, :].rearrange("p a b -> p (a b)") for w in (w_hi, w_lo))
                    V_.tensor_tensor(lo, ps_t[:, n % 2, 0:len(bl) * P], hi.bitcast(F32), ALU.subtract
                                     ).then_inc(su_done, 1)
                dve.wait_ge(ld_vec, 16 * LD_VEC)
                dve.wait_ge(const_made, 1)
                V_.tensor_copy(msg_bias[0:1, :], bias_n[0:1, :])
                V_.tensor_copy(bias_r[32:33, :], bias_n[32:33, :]).then_inc(dve_setup, 1)
                dve.wait_ge(dve_setup, 1)
                V_.tensor_tensor(msg_bias[32:33, :], bias_n[32:33, :], bias_r[32:33, :].bitcast(F32), ALU.subtract)
                dve.wait_ge(iv_ready, 1)
                V_.tensor_tensor(rz_sum[:, :], vec[:, V_IH:V_IH + 2], vec[:, V_HH:V_HH + 2], ALU.add)
                V_.tensor_tensor(scale12[:, :], vec[:, V_G1:V_G2 + 1:4], iv[:, :], ALU.mult).then_inc(dve_setup, 1)
                dve.wait_ge(dve_setup, 2)
                V_.tensor_scalar(rz_bias[:, :], rz_sum[:, :], 0.5, None, ALU.mult)
                V_.tensor_scalar(minus_scale[:, :], scale12[:, 1:2], -1.0, None, ALU.mult)
                V_.tensor_tensor(ms[:, :], vec[:, V_M1:V_M2 + 1:4], scale12[:, :], ALU.mult).then_inc(dve_setup, 1)
                dve.wait_ge(dve_setup, 3)
                V_.tensor_tensor(shift12[:, :], vec[:, V_B1:V_B2 + 1:4], ms[:, :], ALU.subtract
                                 ).then_inc(params_ready, 1)
                V_.memset(fence[:, 3:4], 0.0).then_inc(su_done, 1)

            def moments(src, st, mv, stats, made, g, layer):
                for b in range(G):
                    V_.bn_stats(st[:, b], src[:, b]).then_inc(stats, 1)
                groups(dve, stats, g, G)
                V_.memset(fence[:, layer:layer + 1], 0.0)
                for b in range(G):
                    last = V_.bn_aggr(mv[:, b], st[:, b])
                last.then_inc(made, 1)

            def normalise(dst, src, mv, rs, made):
                for b in range(G):
                    last = V_.tensor_scalar(dst[:, b], src[:, b], mv[:, b, 0:1], rs[:, b:b + 1],
                                            ALU.subtract, ALU.mult)
                last.then_inc(made, 1)

            def moments_1(g, parity):
                landed(dve, x_in, g, parity)
                groups(dve, rstd1_made, g - 1)
                moments(xt[:, parity], st1, mv1, stats1, moments1, g, 0)

            def normalise_1(g, parity):
                groups(dve, rstd1_made, g)
                groups(dve, hT_full, g - 1)
                normalise(xn1, xt[:, parity], mv1, rstd1, xn1_made)

            def mask(g, parity):
                landed(dve, adj_in, g, parity)
                V_.tensor_scalar(neg[:, :, :], adj_t[:, parity], 0.0, MASKED, ALU.is_equal, ALU.mult
                                 ).then_inc(mask_made, 1)

            def step(t, q):
                l, p = t - 1, t + 1
                first = isinstance(t, int) and t == -2
                if first:
                    moments_1(0, 0)
                    normalise_1(0, 0)
                    return
                def add_edge(g, b):
                    if has(g):
                        count(dve, scores_full, g * G + (b + 1))
                        count(dve, edge_made, g * G + (b + 1))
                        V_.tensor_tensor(prob[:, b].rearrange("p (r a) n -> p r (a n)", r=RT),
                                         ps_scores[b],
                                         prob[:, b].rearrange("p (r a) n -> p r (a n)", r=RT), ALU.add
                                         ).then_inc(edge_added, 1)

                y_halves, res_halves = (a[:, :].rearrange("p (b m e) -> p b m e", b=G, e=2) for a in (y, res))

                def even_columns():
                    if not has(l):
                        return
                    groups(dve, even_full, l)
                    groups(dve, odd_made, l)
                    V_.tensor_tensor(odd_sub[:, :, :], ps_even, odd[:, :, 1:HALF + 1], ALU.add)
                    groups(dve, c_lo_made, l - 1)
                    groups(dve, c_hi_made, l - 1)
                    V_.tensor_tensor(y_halves[:, :, :, 0], ps_even, odd[:, :, 0:HALF], ALU.add
                                     ).then_inc(odd_added, 1)
                    groups(dve, odd_added, l)
                    groups(dve, res_made, l)
                    V_.scalar_tensor_tensor(odd_res[:, :, :], odd_sub[:, :, :], minus_scale[:, :],
                                            res_halves[:, :, :, 1], ALU.mult, ALU.add).then_inc(odd_res_made, 1)
                    V_.scalar_tensor_tensor(y_halves[:, :, :, 0], y_halves[:, :, :, 0], scale12[:, 1:2],
                                            res_halves[:, :, :, 0], ALU.mult, ALU.add)

                def low_qk(n):
                    if has(p):
                        groups(dve, qk_hi_made[n], p)
                        V_.tensor_tensor(qk_split[n][:, 1], ps_qk[n], qk_split[n][:, 0].bitcast(F32), ALU.subtract
                                         ).then_inc(qk_lo_made[n], 1)

                def row_max(g, b):
                    if has(g):
                        count(dve, edge_added, g * G + (b + 1))
                        V_.reduce_max(smax[:, b], prob[:, b], AX_X).then_inc(max_made, 1)
                        count(dve, max_made, g * G + (b + 1))
                        V_.tensor_scalar(minus_max[:, b], smax[:, b], -1.0, None, ALU.mult
                                         ).then_inc(max_negated, 1)

                def scale(g, b):
                    if has(g):
                        count(dve, exp_made, g * G + (b + 1))
                        V_.reciprocal(rden[:, b], sums[:, b]).then_inc(rden_made, 1)
                        count(dve, rden_made, g * G + (b + 1))
                        V_.tensor_tensor(prob[:, b], prob[:, b], rden[:, b].unsqueeze(2).broadcast_to([P, H, P]),
                                         ALU.mult).then_inc(scaled, 1)

                if has(l):
                    groups(dve, h2_made, l)
                    groups(dve, z_full, l - 1)
                    V_.tensor_tensor(h2_lo[:, :], h2[:, 1 - q], h2_hi[:, :].bitcast(F32), ALU.subtract
                                     ).then_inc(h2_lo_made, 1)
                if has(l - 1):
                    groups(dve, rg_made, l - 1)
                    groups(dve, gin_full, l - 1)
                    groups(dve, nn_made, l - 2)
                    V_.tensor_tensor(cand[:, :], ps_gin, rg[:, :], ALU.add).then_inc(cand_made, 1)
                if has(p):
                    groups(dve, hT_made, p)
                    groups(dve, v_full, p - 1)
                    V_.tensor_tensor(hT_lo[:, :], hT[:, :], hT_hi[:, :].bitcast(F32), ALU.subtract
                                     ).then_inc(hT_lo_made, 1)
                add_edge(t, 1)
                if has(p):
                    groups(dve, edge_made, t, G)
                    mask(p, 1 - q)
                low_qk(0)
                low_qk(1)
                row_max(t, 1)
                scale(t, 0)
                add_edge(t, 2)
                row_max(t, 2)
                scale(t, 1)
                add_edge(t, 3)
                row_max(t, 3)
                scale(t, 2)
                if has(l):
                    groups(dve, near_made, l)
                    groups(dve, adjT_made, l)
                    V_.tensor_tensor(AT[:, :, :].rearrange("p b n -> p (b n)"),
                                     AT[:, :, :].rearrange("p b n -> p (b n)"), near[:, :], ALU.mult
                                     ).then_inc(AT_made, 1)
                if has(t - 2):
                    groups(dve, outT_full, t - 2)
                    count(dve, out_st[q], (t - 2 - q) * 8)
                    V_.tensor_tensor(out_t[:, q].rearrange("p b n -> p (b n)"), ps_outT,
                                     x2[:, q].rearrange("p b n -> p (b n)"), ALU.add).then_inc(out_made, 1)
                even_columns()
                scale(t, 3)
                if has(l):
                    groups(dve, n_hi_made, l)
                    groups(dve, gin_full, l - 1)
                    V_.tensor_tensor(n_lo[:, :], ps_nmp, n_hi[:, :].bitcast(F32), ALU.subtract
                                     ).then_inc(n_lo_made, 1)
                if has(t + 2):
                    moments_1(t + 2, q)
                if isinstance(t, int) and t == -1:
                    setup()
                add_edge(p, 0)
                row_max(p, 0)
                if has(t):
                    groups(dve, wo_full, t)
                    dve.wait_ge(xr_in, t * 16 + 16)
                    V_.tensor_tensor(x2[:, q].rearrange("p b n -> p (b n)"), ps_wo,
                                     xr[:, :, :].rearrange("p b n -> p (b n)"), ALU.add).then_inc(x2_made, 1)
                if has(l):
                    groups(dve, conv2_full, l)
                    groups(dve, odd_res_made, l)
                    V_.scalar_tensor_tensor(y_halves[:, :, :, 1], ps_pairs, scale12[:, 1:2], odd_res[:, :, :],
                                            ALU.mult, ALU.add).then_inc(y_made, 1)
                if has(t):
                    groups(dve, x2_made, t)
                    moments(x2[:, q], st2, mv2, stats2, moments2, t, 1)
                if has(l):
                    groups(dve, c_hi_made, l)
                    groups(dve, gin_full, l - 1)
                    V_.scalar_tensor_tensor(c_lo[:, :], y[:, :], 0.0, c_hi[:, :].bitcast(F32),
                                            ALU.max, ALU.subtract).then_inc(c_lo_made, 1)
                if has(t + 2):
                    normalise_1(t + 2, q)
                if has(t):
                    groups(dve, rstd2_made, t)
                    groups(dve, h2T_full, t - 1)
                    normalise(xn2, x2[:, q], mv2, rstd2, xn2_made)
                if has(l):
                    groups(dve, r_tanh_made, l)
                    V_.tensor_scalar(rz[:, 0], rz[:, 0], 0.5, 0.5, ALU.mult, ALU.add).then_inc(r_made, 1)
                if has(l):
                    groups(dve, z_tanh_made, l)
                    V_.tensor_scalar(one_z[:, :], rz[:, 1], -0.5, 0.5, ALU.mult, ALU.add)
                    V_.tensor_scalar(rz[:, 1], rz[:, 1], 0.5, 0.5, ALU.mult, ALU.add).then_inc(z_made, 1)

            run(dve, step)

        @block.tensor
        def _(pe):
            mm = nc.tensor.matmul

            pe.wait_ge(ident_made, 2)
            pe.wait_ge(ld_qk, 32)
            for n, w in enumerate((wq_n, wk_n)):
                nc.tensor.transpose(ps_t[:, n, 0:P], w, ident[:, :]).then_inc(su_full, 1)
            pe.wait_ge(su_done, 2)

            def setup():
                for n in range(2, SU):
                    pe.wait_ge(su_done, n - 1)
                    if n == 2:
                        pe.wait_ge(ld_w1, 64)
                        src = [wv_n, wo_n, msg_n]
                    elif n < SU - 1:
                        src = [block_src.get(i) or pair_src[i] for i in batches[n - 3]]
                        if n == 3:
                            pe.wait_ge(ld_w2, 80)
                        if W_TAP in batches[n - 3]:
                            pe.wait_ge(ld_c2, 16)
                    else:
                        pe.wait_ge(ld_vec, 16 * LD_VEC)
                        src = [vec_n]
                    for i, w in enumerate(src):
                        dst = ps_t[:, n % 2, i * P:(i + 1) * P]
                        if isinstance(w, tuple):
                            mm(dst, w[0], ident[:, :], start=True, stop=False)
                            last = mm(dst, w[1], ident[:, :], start=False, stop=True)
                        else:
                            last = nc.tensor.transpose(dst, w, ident[:, :])
                    last.then_inc(su_full, 1)
                pe.wait_ge(su_done, SU)
                pe.wait_ge(const_made, 1)

            def product(dst, pairs):
                ops = [(w, m) for (wh, wl), (mh, ml) in pairs for w, m in ((wh, mh), (wh, ml), (wl, mh))]
                for i, (w, m) in enumerate(ops):
                    last = mm(dst, w, m, start=i == 0, stop=i == len(ops) - 1)
                return last

            def W(i):
                return w_hi[:, i, :], w_lo[:, i, :]

            def transposes(dst, src):
                for b in range(G):
                    last = nc.tensor.transpose(dst[:, b * P:(b + 1) * P], src[:, b], ident[:, :])
                return last

            def step(t, q):
                l, p = t - 1, t + 1
                hT_parts = hT_hi[:, :], hT_lo[:, :]
                h2T = h2_hi[:, :], h2_lo[:, :]

                def scores(g, b, parity):
                    if not has(g):
                        return
                    if b == 0:
                        groups(pe, qk_stacked, g, 10 * 16)
                        groups(pe, probT_made, g - 1, 2 * G)
                    if b == 1:
                        groups(pe, ghn_made, g - 2)
                        groups(pe, x2_made, g - 1)
                    if b == 2:
                        groups(pe, qk_lo_made[1], g + 1)
                        groups(pe, qk_lo_made[0], g + 1)
                        groups(pe, aT_made, g - 1)
                        groups(pe, r_tanh_made, g - 2)
                        groups(pe, cand_made, g - 2)
                    if b == 3:
                        count(pe, edge_added, g * G + 2)
                    for slot in range(SLOTS):
                        for tile in range(RT):
                            rows = slice(64 * tile, 64 * tile + 64)
                            last = mm(ps_scores[b][:, tile, slot * P:(slot + 1) * P],
                                      Q[rows, parity, slot, b, :], K[rows, parity, slot, b, :], start=True, stop=True)
                    last.then_inc(scores_full, 1)

                def project(n):
                    if not has(p):
                        return
                    groups(pe, hT_lo_made, p)
                    if n == 0:
                        groups(pe, qk_lo_made[0], p - 1)
                        groups(pe, cand_made, l - 1)
                    product(ps_qk[n], [(tuple(w[:, n].rearrange("p d h -> p (d h)") for w in (qk_hi, qk_lo)),
                                        hT_parts)]).then_inc(qk_full[n], 1)

                def taps(dst, blocks, hi, lo, at, width, step_, first, last_):
                    for k in range(first, last_):
                        for i, (w, m) in enumerate(((w_hi, hi), (w_hi, lo), (w_lo, hi))):
                            a = at + step_ * k
                            last = mm(dst, w[:, blocks[k], :], m[:, :, a:a + step_ * (width - 1) + 1:step_],
                                      start=k + i == 0, stop=k == len(blocks) - 1 and i == 2)
                    return last

                def odd_taps():
                    if has(l):
                        groups(pe, h1_lo_made, l)
                        blocks = [W_TAP + 2 * k + 1 for k in range(ODD_TAPS)]
                        taps(ps_odd, blocks, h1_hi, h1_lo, 1, HALF + 2, 2, 0, ODD_TAPS).then_inc(odd_full, 1)

                def even_taps(first, last_):
                    if has(l):
                        if first == 0:
                            groups(pe, msg_made, l)
                        blocks = [W_TAP + 2 * k for k in range(EVEN_TAPS)]
                        last = taps(ps_even, blocks, h1_hi, h1_lo, 0, HALF, 2, first, last_)
                        if last_ == EVEN_TAPS:
                            last.then_inc(even_full, 1)

                def pair_taps(first, last_):
                    if has(l):
                        if first == 0:
                            groups(pe, odd_added, l)
                            groups(pe, pair_lo_made, l)
                        blocks = [W_TAP] + [W_PAIR + k - 1 for k in range(1, EVEN_TAPS)]
                        last = taps(ps_pairs, blocks, pair_hi, pair_lo, 0, HALF, 1, first, last_)
                        if last_ == EVEN_TAPS:
                            last.then_inc(conv2_full, 1)

                def flip(b):
                    if not has(t):
                        return
                    if b == 0:
                        groups(pe, u_made, l)
                        groups(pe, v_made, t)
                    count(pe, scaled, t * G + (b + 1))
                    for k in range(2):
                        count(pe, probT_made, t * (2 * G) + (2 * b + k - 1))
                        for i in range(4):
                            last = nc.tensor.transpose(ps_t[:, k, i * P:(i + 1) * P], prob[:, b, 4 * k + i],
                                                       ident[:, :])
                        last.then_inc(probT_full, 1)

                def weigh(b):
                    if not has(t):
                        return
                    count(pe, probT_made, t * (2 * G) + (2 * b + 2))
                    count(pe, edge_added, t * G + G)
                    for k in range(H // 2):
                        for e in range(2):
                            last = mm(ps_av[2 * HD * k:2 * HD * (k + 1), b * P:(b + 1) * P],
                                      v_pad[:, b, k, 2 * e:2 * e + 2, :].rearrange("p f d -> p (f d)"),
                                      probT[:, b % 2, 2 * k + e], start=e == 0, stop=e == 1)
                    last.then_inc(av_full, 1)

                def three(dst, weight, moving, first, last_):
                    w, (hi, lo) = W(weight), moving
                    mm(dst, w[0], hi, start=first, stop=False)
                    mm(dst, w[0], lo, start=False, stop=False)
                    return mm(dst, w[1], hi, start=False, stop=last_)

                n_parts, c_parts = (n_hi[:, :], n_lo[:, :]), (c_hi[:, :], c_lo[:, :])

                if has(l):
                    groups(pe, xn2_made, l)
                    groups(pe, y_made, l - 1)
                    transposes(ps_h2T, xn2).then_inc(h2T_full, 1)
                    if has(t):
                        count(pe, edge_added, t * G + 1)
                    groups(pe, probT_made, t - 1, 2 * G)
                    transposes(ps_adjT, adj_t[:, 1 - q]).then_inc(adjT_full, 1)
                if has(t):
                    count(pe, edge_added, t * G + 1)
                    for b in range(G):
                        sl = slice(b * P, (b + 1) * P)
                        last = mm(ps_v[:, sl], hT[:, sl], w_full[:, W_V, :], start=True, stop=True)
                    last.then_inc(v_full, 1)
                if has(p):
                    groups(pe, xn1_made, p)
                    groups(pe, qk_lo_made[1], p - 1)
                    groups(pe, aT_made, t - 1)
                    groups(pe, r_tanh_made, l - 1)
                    transposes(ps_hT, xn1).then_inc(hT_full, 1)
                scores(t, 1, q)
                if has(l):
                    groups(pe, h2_lo_made, l)
                    groups(pe, z_tanh_made, l - 1)
                    product(ps_conv1, [(W(W_C1), h2T)]).then_inc(conv1_full, 1)
                    groups(pe, adjT_made, l)
                    product(ps_s3, [(W(W_S), h2T)]).then_inc(s_full, 1)
                project(0)
                project(1)
                if has(l):
                    mm(ps_msg, ones2[:, :], msg_bias[:, :].unsqueeze(1).broadcast_to([P, G, P]),
                       start=True, stop=True)
                    for b in range(G):
                        sl = slice(b * P, (b + 1) * P)
                        last = mm(ps_msg[:, sl], h2[:, 1 - q, sl], w_full[:, W_MSG, :], start=False, stop=True,
                                  skip_group_check=True)
                    last.then_inc(msg_full, 1)
                odd_taps()
                scores(t, 2, q)
                scores(t, 3, q)
                flip(0)
                even_taps(0, 5)
                if has(l):
                    groups(pe, odd_made, l)
                    count(pe, v_rows, l * 32 + 32)
                    for b in range(G):
                        last = mm(ps_dist[:, b * P:(b + 1) * P], U[:, b], V[:, b], start=True, stop=True)
                    last.then_inc(dist_full, 1)
                flip(1)
                even_taps(5, EVEN_TAPS)
                weigh(0)
                if has(t - 2):
                    groups(pe, oT_made, t - 2)
                    groups(pe, edge_added, t, G)
                    groups(pe, x2_made, t - 1)
                    transposes(ps_outT, oT).then_inc(outT_full, 1)
                weigh(1)
                flip(2)
                if has(l):
                    groups(pe, AT_made, l)
                    for b in range(G):
                        last = mm(ps_nmp[:, b * P:(b + 1) * P], msg[:, b], AT[:, b], start=True, stop=True)
                    last.then_inc(nmp_full, 1)
                pair_taps(0, 3)
                if has(l):
                    groups(pe, edge_added, t, G)
                    groups(pe, ghn_made, l - 1)
                    three(ps_ghn, W_HN, h2T, True, True).then_inc(ghn_full, 1)
                weigh(2)
                flip(3)
                pair_taps(3, 6)
                if isinstance(t, int) and t == -1:
                    setup()
                scores(p, 0, 1 - q)
                weigh(3)
                pair_taps(6, 7)
                if has(t):
                    groups(pe, aT_made, t)
                    groups(pe, out_made, t - 2)
                    for b in range(G):
                        sl = slice(b * P, (b + 1) * P)
                        last = mm(ps_wo[:, sl], aT[:, sl], w_full[:, W_O, :], start=True, stop=True)
                    last.then_inc(wo_full, 1)
                pair_taps(7, EVEN_TAPS)
                if has(l):
                    groups(pe, n_lo_made, l)
                    three(ps_z, W_HZ, h2T, True, False)
                    groups(pe, r_tanh_made, l - 1)
                    three(ps_r, W_HR, h2T, True, False)
                    three(ps_r, W_IR1, n_parts, False, False)
                    three(ps_z, W_IZ1, n_parts, False, False)
                    groups(pe, c_lo_made, l)
                    three(ps_r, W_IR0, c_parts, False, True).then_inc(r_full, 1)
                    three(ps_z, W_IZ0, c_parts, False, True).then_inc(z_full, 1)
                    groups(pe, edge_added, t, G)
                    groups(pe, cand_made, l - 1)
                    three(ps_gin, W_IN1, n_parts, True, False)
                    three(ps_gin, W_IN0, c_parts, False, True).then_inc(gin_full, 1)

            run(pe, step)


_INS = ['x', 'adj', 'L0_gnn_W_q', 'L0_gnn_W_k', 'L0_gnn_W_v', 'L0_gnn_W_e', 'L0_gnn_W_o', 'L1_gnn_w_se',
        'L1_gnn_b_se', 'L1_gnn_conv1_w', 'L1_gnn_bn1_g', 'L1_gnn_bn1_b', 'L1_gnn_bn1_m', 'L1_gnn_bn1_v',
        'L1_gnn_conv2_w', 'L1_gnn_bn2_g', 'L1_gnn_bn2_b', 'L1_gnn_bn2_m', 'L1_gnn_bn2_v', 'L1_gnn_w_msg',
        'L1_gnn_b_msg', 'L1_gnn_w_ih', 'L1_gnn_b_ih', 'L1_gnn_w_hh', 'L1_gnn_b_hh']
_OUTS = [((64, 128, 128), 'float32')]


def kernel(**inputs):
    import numpy as _np
    import concourse.bacc as _bacc
    from concourse import mybir as _mybir
    from concourse.bass_utils import run_bass_kernel_spmd as _run

    nc = _bacc.Bacc("TRN2", target_bir_lowering=False, num_devices=1)
    arrays, args = {}, []
    for name in _INS:
        a = _np.ascontiguousarray(inputs[name])
        arrays[f"in_{name}_dram"] = a
        args.append(nc.dram_tensor(f"in_{name}_dram", a.shape, _mybir.dt.from_np(a.dtype), kind="ExternalInput").ap())
    for i, (shape, dtype) in enumerate(_OUTS):
        dt = _mybir.dt.from_np(_np.dtype(dtype))
        args.append(nc.dram_tensor(f"out_{i}_dram", shape, dt, kind="ExternalOutput").ap())
    build(nc, *args)
    r = _run(nc, [arrays], core_ids=[0])
    got = tuple(r.results[0][f"out_{i}_dram"] for i in range(len(_OUTS)))
    return got[0]
```
